# Optimizing a Trainium2 kernel written in Bass

```python
import numpy as np
import jax
import jax.numpy as jnp

def _softmax(x, axis=-1):
    return jax.nn.softmax(x, axis=axis)

def _gelu(x):
    return jax.nn.gelu(x, approximate=True)

def _silu(x):
    return jax.nn.silu(x)

def _sigmoid(x):
    return jax.nn.sigmoid(x)

def _layernorm(x, axis=-1, eps=1e-05):
    m = jnp.mean(x, axis=axis, keepdims=True)
    v = jnp.var(x, axis=axis, keepdims=True)
    return (x - m) / jnp.sqrt(v + eps)

def _scatter_add(tgt, idx, src, axis=0):
    return tgt.at[idx].add(src)

def _segment_sum(src, seg, n):
    return jax.ops.segment_sum(src, seg, n)
kernel_name = 'mk_seq_postln_d1_jaxref_r8_0970cf'

def setup_inputs(seed: int=0):
    np.random.seed(seed)
    _w = jnp.asarray

    def _L0_attn_setup():
        import jax, jax.numpy as jnp
        import numpy as np
        B, L, D, H, F = (2, 128, 128, 16, 512)
        DH = D // H
        EPS = 1e-06

        def _layernorm(x, g, b, eps=1e-05):
            m = jnp.mean(x, axis=-1, keepdims=True)
            v = jnp.mean((x - m) ** 2, axis=-1, keepdims=True)
            return (x - m) / jnp.sqrt(v + eps) * g + b

        def _decoder_layer(inputs, Wq, bq, Wk, bk, Wv, bv, Wo, bo, ln1_g, ln1_b, W1, b1, W2, b2, ln2_g, ln2_b):
            Bn, Ln, Dn = inputs.shape

            def heads(W, b):
                return (inputs @ W + b).reshape(Bn, Ln, H, DH).transpose(0, 2, 1, 3)
            q = jax.nn.sigmoid(heads(Wq, bq))
            k = jax.nn.sigmoid(heads(Wk, bk))
            v = heads(Wv, bv)
            normal = (jnp.arange(Ln, dtype=jnp.float32) + 1.0)[None, None, :]
            sink_in = normal / jnp.einsum('bhld,bhld->bhl', q + EPS, jnp.cumsum(k, axis=2) + EPS)
            src_out = normal / jnp.einsum('bhld,bhld->bhl', k + EPS, jnp.cumsum(q, axis=2) + EPS)
            cons_sink = jnp.einsum('bhld,bhld->bhl', q + EPS, jnp.cumsum(k * src_out[..., None], axis=2) + EPS) / normal
            cons_src = jnp.einsum('bhld,bhld->bhl', k + EPS, jnp.cumsum(q * sink_in[..., None], axis=2) + EPS) / normal
            cons_src = jnp.clip(cons_src, -1.0, 1.0)
            sink_alloc = jax.nn.sigmoid(cons_sink)
            cons_src = jnp.exp(cons_src)
            src_comp = cons_src / jnp.cumsum(cons_src, axis=-1) * normal
            qs = q * (sink_in / normal)[..., None]
            vs = v * src_comp[..., None]
            kv = jnp.cumsum(jnp.einsum('bhld,bhlm->bhldm', k, vs), axis=2)
            x = jnp.einsum('bhld,bhldm->bhlm', qs, kv) * sink_alloc[..., None]
            x = x.transpose(0, 2, 1, 3).reshape(Bn, Ln, Dn)
            attn = x @ Wo + bo
            h = _layernorm(inputs + attn, ln1_g, ln1_b)
            ffn = jax.nn.gelu(h @ W1 + b1, approximate=False) @ W2 + b2
            return _layernorm(h + ffn, ln2_g, ln2_b)
        key = jax.random.key(seed)
        ks = jax.random.split(key, 12)

        def w(k, shape):
            return jax.random.normal(k, shape, dtype=jnp.float32) * 0.02
        return {'inputs': jax.random.normal(ks[0], (B, L, D), dtype=jnp.float32), 'attn_mask': jnp.zeros((L, L), dtype=jnp.bool_), 'Wq': w(ks[1], (D, D)), 'bq': jnp.zeros((D,), jnp.float32), 'Wk': w(ks[2], (D, D)), 'bk': jnp.zeros((D,), jnp.float32), 'Wv': w(ks[3], (D, D)), 'bv': jnp.zeros((D,), jnp.float32), 'Wo': w(ks[4], (D, D)), 'bo': jnp.zeros((D,), jnp.float32), 'ln1_g': jnp.ones((D,), jnp.float32), 'ln1_b': jnp.zeros((D,), jnp.float32), 'W1': w(ks[5], (D, F)), 'b1': jnp.zeros((F,), jnp.float32), 'W2': w(ks[6], (F, D)), 'b2': jnp.zeros((D,), jnp.float32), 'ln2_g': jnp.ones((D,), jnp.float32), 'ln2_b': jnp.zeros((D,), jnp.float32)}
    _L0_attn_in = _L0_attn_setup()

    def _L0_ffn_setup():
        import jax, jax.numpy as jnp
        import numpy as np
        B, S, D_MODEL, D_FF, E, R, TOP_K = (4, 256, 128, 512, 8, 16, 2)
        key = jax.random.key(seed)
        ks = jax.random.split(key, 9)
        sd = 1.0 / np.sqrt(D_MODEL)
        return {'hidden_states': jax.random.normal(ks[0], (B, S, D_MODEL), jnp.float32), 'wi': jax.random.normal(ks[1], (D_FF, D_MODEL), jnp.float32) * sd, 'bi': jax.random.normal(ks[2], (D_FF,), jnp.float32) * 0.01, 'wo': jax.random.normal(ks[3], (D_MODEL, D_FF), jnp.float32) * (1.0 / np.sqrt(D_FF)), 'bo': jax.random.normal(ks[4], (D_MODEL,), jnp.float32) * 0.01, 'lora_A': jax.random.normal(ks[5], (E, R, D_MODEL), jnp.float32) * sd, 'lora_B': jax.random.normal(ks[6], (E, D_FF, R), jnp.float32) * 0.02, 'gate_w': jax.random.normal(ks[7], (E, D_MODEL), jnp.float32) * sd, 'gate_b': jax.random.normal(ks[8], (E,), jnp.float32) * 0.01}
    _L0_ffn_in = _L0_ffn_setup()
    _d = {'L0_attn_inputs': _L0_attn_in['inputs'], 'L0_attn_attn_mask': _L0_attn_in['attn_mask'], 'L0_attn_Wq': _L0_attn_in['Wq'], 'L0_attn_bq': _L0_attn_in['bq'], 'L0_attn_Wk': _L0_attn_in['Wk'], 'L0_attn_bk': _L0_attn_in['bk'], 'L0_attn_Wv': _L0_attn_in['Wv'], 'L0_attn_bv': _L0_attn_in['bv'], 'L0_attn_Wo': _L0_attn_in['Wo'], 'L0_attn_bo': _L0_attn_in['bo'], 'L0_attn_ln1_g': _L0_attn_in['ln1_g'], 'L0_attn_ln1_b': _L0_attn_in['ln1_b'], 'L0_attn_W1': _L0_attn_in['W1'], 'L0_attn_b1': _L0_attn_in['b1'], 'L0_attn_W2': _L0_attn_in['W2'], 'L0_attn_b2': _L0_attn_in['b2'], 'L0_attn_ln2_g': _L0_attn_in['ln2_g'], 'L0_attn_ln2_b': _L0_attn_in['ln2_b'], 'L0_ffn_wi': _L0_ffn_in['wi'], 'L0_ffn_bi': _L0_ffn_in['bi'], 'L0_ffn_wo': _L0_ffn_in['wo'], 'L0_ffn_bo': _L0_ffn_in['bo'], 'L0_ffn_lora_A': _L0_ffn_in['lora_A'], 'L0_ffn_lora_B': _L0_ffn_in['lora_B'], 'L0_ffn_gate_w': _L0_ffn_in['gate_w'], 'L0_ffn_gate_b': _L0_ffn_in['gate_b']}
    _x0 = _d['L0_attn_inputs']
    _d['L0_attn_inputs'] = jax.random.normal(jax.random.fold_in(jax.random.key(seed), 1), (4, 1024, 128), dtype=_x0.dtype)
    del _x0
    return _d

def reference(L0_attn_inputs, L0_attn_attn_mask, L0_attn_Wq, L0_attn_bq, L0_attn_Wk, L0_attn_bk, L0_attn_Wv, L0_attn_bv, L0_attn_Wo, L0_attn_bo, L0_attn_ln1_g, L0_attn_ln1_b, L0_attn_W1, L0_attn_b1, L0_attn_W2, L0_attn_b2, L0_attn_ln2_g, L0_attn_ln2_b, L0_ffn_wi, L0_ffn_bi, L0_ffn_wo, L0_ffn_bo, L0_ffn_lora_A, L0_ffn_lora_B, L0_ffn_gate_w, L0_ffn_gate_b):

    def _L0_attn_ref(inputs, attn_mask, Wq, bq, Wk, bk, Wv, bv, Wo, bo, ln1_g, ln1_b, W1, b1, W2, b2, ln2_g, ln2_b):
        import jax, jax.numpy as jnp
        import numpy as np
        B, L, D, H, F = (2, 128, 128, 16, 512)
        DH = D // H
        EPS = 1e-06

        def _layernorm(x, g, b, eps=1e-05):
            m = jnp.mean(x, axis=-1, keepdims=True)
            v = jnp.mean((x - m) ** 2, axis=-1, keepdims=True)
            return (x - m) / jnp.sqrt(v + eps) * g + b

        def _decoder_layer(inputs, Wq, bq, Wk, bk, Wv, bv, Wo, bo, ln1_g, ln1_b, W1, b1, W2, b2, ln2_g, ln2_b):
            Bn, Ln, Dn = inputs.shape

            def heads(W, b):
                return (inputs @ W + b).reshape(Bn, Ln, H, DH).transpose(0, 2, 1, 3)
            q = jax.nn.sigmoid(heads(Wq, bq))
            k = jax.nn.sigmoid(heads(Wk, bk))
            v = heads(Wv, bv)
            normal = (jnp.arange(Ln, dtype=jnp.float32) + 1.0)[None, None, :]
            sink_in = normal / jnp.einsum('bhld,bhld->bhl', q + EPS, jnp.cumsum(k, axis=2) + EPS)
            src_out = normal / jnp.einsum('bhld,bhld->bhl', k + EPS, jnp.cumsum(q, axis=2) + EPS)
            cons_sink = jnp.einsum('bhld,bhld->bhl', q + EPS, jnp.cumsum(k * src_out[..., None], axis=2) + EPS) / normal
            cons_src = jnp.einsum('bhld,bhld->bhl', k + EPS, jnp.cumsum(q * sink_in[..., None], axis=2) + EPS) / normal
            cons_src = jnp.clip(cons_src, -1.0, 1.0)
            sink_alloc = jax.nn.sigmoid(cons_sink)
            cons_src = jnp.exp(cons_src)
            src_comp = cons_src / jnp.cumsum(cons_src, axis=-1) * normal
            qs = q * (sink_in / normal)[..., None]
            vs = v * src_comp[..., None]
            kv = jnp.cumsum(jnp.einsum('bhld,bhlm->bhldm', k, vs), axis=2)
            x = jnp.einsum('bhld,bhldm->bhlm', qs, kv) * sink_alloc[..., None]
            x = x.transpose(0, 2, 1, 3).reshape(Bn, Ln, Dn)
            attn = x @ Wo + bo
            h = _layernorm(inputs + attn, ln1_g, ln1_b)
            ffn = jax.nn.gelu(h @ W1 + b1, approximate=False) @ W2 + b2
            return _layernorm(h + ffn, ln2_g, ln2_b)
        return _decoder_layer(inputs, Wq, bq, Wk, bk, Wv, bv, Wo, bo, ln1_g, ln1_b, W1, b1, W2, b2, ln2_g, ln2_b)

    def _L0_ffn_ref(hidden_states, wi, bi, wo, bo, lora_A, lora_B, gate_w, gate_b):
        import jax, jax.numpy as jnp
        import numpy as np
        B, S, D_MODEL, D_FF, E, R, TOP_K = (4, 256, 128, 512, 8, 16, 2)
        logits = jnp.einsum('bsd,ed->bse', hidden_states, gate_w) + gate_b
        scores = jax.nn.softmax(logits, axis=-1)
        top_v, top_i = jax.lax.top_k(scores, TOP_K)
        val_sum = top_v.sum(axis=-1)
        out = jnp.zeros_like(hidden_states)
        for e in range(E):
            count = (top_i == e).sum(axis=-1).astype(hidden_states.dtype)
            gate = count * val_sum
            inter = jnp.einsum('bsd,fd->bsf', hidden_states, wi) + bi + jnp.einsum('bsr,fr->bsf', jnp.einsum('bsd,rd->bsr', hidden_states, lora_A[e]), lora_B[e])
            h = jax.nn.relu(inter)
            expert_out = jnp.einsum('bsf,df->bsd', h, wo) + bo
            out = out + gate[..., None] * expert_out
        return out
    x = L0_attn_inputs
    x = _layernorm(x + _L0_attn_ref(x, L0_attn_attn_mask, L0_attn_Wq, L0_attn_bq, L0_attn_Wk, L0_attn_bk, L0_attn_Wv, L0_attn_bv, L0_attn_Wo, L0_attn_bo, L0_attn_ln1_g, L0_attn_ln1_b, L0_attn_W1, L0_attn_b1, L0_attn_W2, L0_attn_b2, L0_attn_ln2_g, L0_attn_ln2_b), axis=-1)
    x = _layernorm(x + _L0_ffn_ref(x, L0_ffn_wi, L0_ffn_bi, L0_ffn_wo, L0_ffn_bo, L0_ffn_lora_A, L0_ffn_lora_B, L0_ffn_gate_w, L0_ffn_gate_b), axis=-1)
    return x

_drawn_inputs = setup_inputs


def setup_inputs(seed=0):
    import zlib

    import numpy as np

    out = dict(_drawn_inputs(seed))
    spreads = {'L0_attn_bq': (0.0, 2.0),
     'L0_attn_bk': (0.0, 2.0),
     'L0_attn_bv': (0.0, 0.8),
     'L0_attn_bo': (0.0, 0.1),
     'L0_attn_ln1_g': (1.0, 0.2),
     'L0_attn_ln1_b': (0.0, 0.1),
     'L0_attn_b1': (0.0, 0.655),
     'L0_attn_b2': (0.0, 0.1),
     'L0_attn_ln2_g': (1.0, 0.2),
     'L0_attn_ln2_b': (0.0, 0.1)}
    factors = {'L0_attn_Wq': 8.0,
     'L0_attn_Wk': 8.0,
     'L0_attn_Wv': 8.0,
     'L0_attn_Wo': 7.683,
     'L0_ffn_bi': 8.0,
     'L0_ffn_bo': 6.371,
     'L0_ffn_gate_b': 24.258}
    for name, (base, spread) in spreads.items():
        noise = np.random.default_rng([zlib.crc32(name.encode()), seed]).standard_normal(out[name].shape)
        drawn = base * np.exp(spread * noise) if base else spread * noise
        out[name] = jnp.asarray(drawn.astype(out[name].dtype))
    for name, factor in factors.items():
        out[name] = (out[name] * factor).astype(out[name].dtype)
    return out
```

```python
import concourse.bass as bass
from concourse import mybir
from contextlib import ExitStack

F32 = mybir.dt.float32
ALU = mybir.AluOpType
ACT = mybir.ActivationFunctionType
AX_X = mybir.AxisListType.X

P = 128
BATCH, LENGTH = 4, 1024
HEADS, DH = 16, 8
FF = 512
EXPERTS, RANK = 8, 16
TOK = 512
SUB = TOK // P
TILES = BATCH * LENGTH // TOK
FC = FF // P
ATT_EPS = 1e-6
LN_EPS = 1e-5
HW = SUB * HEADS

W_ATT = {"wq": (0, 128), "wk": (128, 256), "wv": (256, 384), "headsum": (384, 400), "cols": (400, 415)}
COLS = {"bq": 0, "bk": 1, "bv": 2, "g1": 3, "b1n": 4, "b1": 5, "bi": 9}
N_COLS = 15
W_CONST = {"ident": (0, 128), "upper": (128, 256), "ones": (256, 384), "norm": (384, 640), "inorm": (640, 896),
           "prefer": (896, 928), "mhalf": (928, 932), "lneps": (932, 936)}
ROWS = {"bo": 0, "g1": 1, "b1n": 2, "b2": 3, "g2": 4, "b2n": 5, "bffn": 6}
W_FFN = {"w1": (0, 512), "w2": (512, 1024)}
W_MOE = {"la": (0, 128), "gate": (128, 136), "wi": (136, 648), "lb": (648, 1160), "wo": (1160, 1672)}


class Tile:

    def __init__(self, pair, c):
        self.pair, self.c = pair, c
        self.n = 2 * pair + c
        self.par = c % 2
        self.slot_uses = pair + c // 2

    def plus(self, k):
        return Tile(self.pair, self.c + k)

    def exists(self):
        return not isinstance(self.n, int) or 0 <= self.n < TILES


def wait(eng, sem, value):
    if isinstance(value, int) and value <= 0:
        return
    eng.wait_ge(sem, value)


def run_steps(eng, step):
    for c in (-1, 0, 1):
        step(Tile(0, c))
    with eng.Fori(1, 3) as pair:
        step(Tile(pair, 0))
        step(Tile(pair, 1))
    for c in (0, 1, 2, 3):
        step(Tile(3, c))


def build(nc, x, x_t, att_w, consts, wo_rep, rows, gate_row, ffn_w, moe_w, out):
    ctx = ExitStack()
    with ctx:
        def sb(name, shape):
            return ctx.enter_context(nc.sbuf_tensor(name, shape, F32))

        def bank(name):
            return ctx.enter_context(nc.psum_tensor(name, [P, TOK], F32))

        def sem(name):
            return ctx.enter_context(nc.semaphore(name))

        s_att = sb("s_att", [P, 415])
        s_con = sb("s_con", [P, 936])
        s_wor = sb("s_wor", [P, DH, P])
        s_row = sb("s_row", [P, 7, P])
        s_gb = sb("s_gb", [P, EXPERTS])
        s_ffn = sb("s_ffn", [P, 2 * FF])
        s_moe = sb("s_moe", [P, 1672])

        def att(name):
            return s_att[:, slice(*W_ATT[name])]

        def col(name, k=0):
            at = W_ATT["cols"][0] + COLS[name] + k
            return s_att[:, at:at + 1]

        def con(name):
            return s_con[:, slice(*W_CONST[name])]

        def moe(name):
            return s_moe[:, slice(*W_MOE[name])]

        def row(name):
            return s_row[:, ROWS[name], :]

        def over_subs(r):
            return r.unsqueeze(1).to_broadcast([P, SUB, P])

        w1 = s_ffn[:, 0:512]
        w2 = s_ffn[:, 512:1024].rearrange("p (f n) -> p f n", f=FC)
        wo = moe("wo").rearrange("p (f n) -> p f n", f=FC)
        ident, upper, ones = con("ident"), con("upper"), con("ones")

        neg_bi = sb("neg_bi", [P, FC])
        r_b1b2 = sb("r_b1b2", [P, P])
        r_cmoe = sb("r_cmoe", [P, P])
        bi_rep = sb("bi_rep", [P, FC, P])
        onesrow = sb("onesrow", [P, TOK])

        xT = [sb(f"xT{i}", [P, TOK]) for i in range(2)]
        xt = [sb(f"xt{i}", [P, SUB, P]) for i in range(2)]
        q, k, v = sb("q", [P, TOK]), sb("k", [P, TOK]), sb("v", [P, TOK])
        cum_k = [sb(f"cum_k{i}", [P, TOK]) for i in range(2)]
        cum_q = [sb(f"cum_q{i}", [P, TOK]) for i in range(2)]
        cum_ks = [sb(f"cum_ks{i}", [P, TOK]) for i in range(2)]
        cum_qs = [sb(f"cum_qs{i}", [P, TOK]) for i in range(2)]
        qk1, kq1 = sb("qk1", [P, TOK]), sb("kq1", [P, TOK])
        qk2, kq2 = qk1, kq1
        k_src, q_sink = sb("k_src", [P, TOK]), sb("q_sink", [P, TOK])
        rden = sb("rden", [P, 2 * HW])
        rden_x = sb("rden_x", [P, 2, HW, DH])
        cons = sb("cons", [P, 2 * HW])
        clipped = sb("clipped", [P, HW])
        tanh_half = sb("tanh_half", [P, HW])
        alloc = sb("alloc", [P, HW])
        fac_x = rden_x[:, 0, :, :]
        esrc = sb("esrc", [P, HW])
        esrc_sum = sb("esrc_sum", [P, HEADS])
        rcum_e, e_norm = sb("rcum_e", [P, HW]), sb("e_norm", [P, HW])
        comp_x = rden_x[:, 1, :, :]
        q_fac = [sb(f"q_fac{i}", [P, TOK]) for i in range(2)]
        vs = sb("vs", [P, TOK])
        vb = sb("vb", [P, DH, TOK])
        kv = sb("kv", [P, 3, TOK])
        cum_kv = [sb(f"cum_kv{i}", [P, DH, TOK]) for i in range(2)]
        prod = sb("prod", [P, 4, TOK])

        x_bo = sb("x_bo", [P, SUB, P])
        x_b2n = sb("x_b2n", [P, SUB, P])
        res = [sb(f"res{i}", [P, SUB, P]) for i in range(4)]
        stats = [sb(f"stats{i}", [P, SUB, 6]) for i in range(4)]
        mv = [sb(f"mv{i}", [P, SUB, 2]) for i in range(4)]
        var_eps = [sb(f"var_eps{i}", [P, SUB]) for i in range(4)]
        rstd = [sb(f"rstd{i}", [P, SUB]) for i in range(4)]
        shift = [sb(f"shift{i}", [P, SUB]) for i in range(4)]
        fence = sb("fence", [P, 1])
        n1, n2 = sb("n1", [P, SUB, P]), sb("n2", [P, SUB, P])
        x2 = [sb(f"x2_{i}", [P, SUB, P]) for i in range(2)]
        y = [sb(f"y{i}", [P, SUB, P]) for i in range(2)]
        hT = sb("hT", [P, TOK])
        h_res = sb("h_res", [P, SUB, P])
        gel = sb("gel", [P, FC, TOK])
        hsum = gel

        x2T = [sb(f"x2T{i}", [P, TOK]) for i in range(2)]
        logit, prob, ex = (sb(n, [P, SUB, EXPERTS]) for n in ("logit", "prob", "ex"))
        prob2, eq, pick = (sb(n, [P, SUB, EXPERTS]) for n in ("prob2", "eq", "pick"))
        first, second, delta = (sb(n, [P, SUB, EXPERTS]) for n in ("first", "second", "delta"))
        m_log, s_ex, r_ex, top1, top2, m_pick = (sb(n, [P, SUB]) for n in ("m_log", "s_ex", "r_ex", "top1", "top2", "m_pick"))
        gate_sum = [sb(f"gate_sum{i}", [P, SUB]) for i in range(2)]
        u1, ud = sb("u1", [P, SUB, P]), sb("ud", [P, SUB, P])
        u1T = [sb(f"u1T{i}", [P, TOK]) for i in range(2)]
        udT = [sb(f"udT{i}", [P, TOK]) for i in range(2)]
        c_gate = sb("c_gate", [P, SUB, P])
        x2c = [sb(f"x2c{i}", [P, SUB, P]) for i in range(2)]
        relu1 = sb("relu1", [P, 2, TOK])

        pA, pB, pS, pO = bank("pA"), bank("pB"), bank("pS"), bank("pO")
        pG = [bank("pG0"), bank("pG1")]
        pY, pM = bank("pY"), bank("pM")
        pO3, pY3, pM3 = (b[:, :].rearrange("p (s n) -> p s n", s=SUB) for b in (pO, pY, pM))
        p_den, p_cons, p_cume = pS[:, 0:2 * HW], pS[:, 2 * HW:4 * HW], pS[:, 4 * HW:5 * HW]
        p_log = pM[:, 0:SUB * EXPERTS].rearrange("p (s e) -> p s e", s=SUB)

        att_loaded, con_loaded = sem("att_loaded"), sem("con_loaded")
        row_loaded, gb_loaded = sem("row_loaded"), sem("gb_loaded")
        moe_loaded = sem("moe_loaded")
        xT_loaded = [sem(f"xT_loaded{i}") for i in range(2)]
        xt_loaded = [sem(f"xt_loaded{i}") for i in range(2)]
        vb_loaded = [sem(f"vb_loaded{m}") for m in range(DH)]
        y_free = [sem(f"y_free{i}") for i in range(2)]
        ones_ready, negbi_ready, rowsum_ready, cmoe_mm, cmoe_ready = (
            sem(n) for n in ("ones_ready", "negbi_ready", "rowsum_ready", "cmoe_mm", "cmoe_ready"))
        q_proj, k_proj, v_proj = sem("q_proj"), sem("k_proj"), sem("v_proj")
        q_ready, k_ready, v_ready = sem("q_ready"), sem("k_ready"), sem("v_ready")
        cumk_ready, cumq_ready = sem("cumk_ready"), sem("cumq_ready")
        qk1_ready, kq1_ready, den_ready = sem("qk1_ready"), sem("kq1_ready"), sem("den_ready")
        rden_ready, rdenx_ready = sem("rden_ready"), sem("rdenx_ready")
        sinkT_ready, srcT_ready = sem("sinkT_ready"), sem("srcT_ready")
        qsink_ready, ksrc_ready = sem("qsink_ready"), sem("ksrc_ready")
        cumks_ready, cumqs_ready = sem("cumks_ready"), sem("cumqs_ready")
        qk2_ready, kq2_ready, consp_ready = sem("qk2_ready"), sem("kq2_ready"), sem("consp_ready")
        cons_ready, clip_ready, tanh_ready, esrc_ready = (sem(n) for n in ("cons_ready", "clip_ready", "tanh_ready", "esrc_ready"))
        alloc_ready, facx_ready, facT_ready, qfac_ready = (sem(n) for n in ("alloc_ready", "facx_ready", "facT_ready", "qfac_ready"))
        cume_ready, rcume_ready, enorm_ready, compx_ready = (sem(n) for n in ("cume_ready", "rcume_ready", "enorm_ready", "compx_ready"))
        esum_ready = sem("esum_ready")
        compT_ready, vs_ready = sem("compT_ready"), sem("vs_ready")
        kv_ready, cumkv_ready, prod_ready, red_ready = (sem(n) for n in ("kv_ready", "cumkv_ready", "prod_ready", "red_ready"))
        res_ready = [sem(f"res_ready{i}") for i in range(4)]
        stats_ready = [sem(f"stats_ready{i}") for i in range(4)]
        mv_ready = [sem(f"mv_ready{i}") for i in range(4)]
        vareps_ready = [sem(f"vareps_ready{i}") for i in range(4)]
        rstd_ready = [sem(f"rstd_ready{i}") for i in range(4)]
        shift_ready = [sem(f"shift_ready{i}") for i in range(4)]
        norm_ready = [sem(f"norm_ready{i}") for i in range(4)]
        xbo_ready, xb2n_ready = sem("xbo_ready"), sem("xb2n_ready")
        hTp_ready, hT_ready, hg_ready, hres_ready = (sem(n) for n in ("hTp_ready", "hT_ready", "hg_ready", "hres_ready"))
        w1_done, gelu_ready, w2_done = sem("w1_done"), sem("gelu_ready"), sem("w2_done")
        zg_ready = sem("zg_ready")
        x2Tp_ready, x2T_ready, logp_ready, up_ready = (sem(n) for n in ("x2Tp_ready", "x2T_ready", "logp_ready", "up_ready"))
        gate_step = sem("gate_step")
        ex_ready = sem("ex_ready")
        gsum_ready = sem("gsum_ready")
        u1_ready, ud_ready, u1Tp_ready, udTp_ready, u1T_ready, udT_ready = (
            sem(n) for n in ("u1_ready", "ud_ready", "u1Tp_ready", "udTp_ready", "u1T_ready", "udT_ready"))
        delta_ready = sem("delta_ready")
        cg_ready, x2c_ready = sem("cg_ready"), sem("x2c_ready")
        in1_done, relu_ready, in2_done, hsum_ready, wo_done = (
            sem(n) for n in ("in1_done", "relu_ready", "in2_done", "hsum_ready", "wo_done"))

        x_v = x.rearrange("(t s p) d -> p t s d", s=SUB, p=P)
        out_v = out.rearrange("(t s p) d -> p t s d", s=SUB, p=P)

        block = ctx.enter_context(nc.Block())

        @block.sync
        def _(sp):
            def load_xT(t):
                wait(sp, v_proj, t.n - 1)
                sp.dma_start(xT[t.par][:, :], x_t[:, bass.ds(t.n * TOK, TOK)]).then_inc(xT_loaded[t.par], 16)

            def load_xt(t):
                wait(sp, xb2n_ready, t.n - 1)
                sp.dma_start(xt[t.par][:, :, :].unsqueeze(1), x_v[:, bass.ds(t.n, 1), :, :]).then_inc(xt_loaded[t.par], 16)

            def spread_vs(t):
                sp.wait_ge(vs_ready, t.n + 1)
                for m in range(DH):
                    src = vs[m:P:DH, :].unsqueeze(1).to_broadcast([HEADS, DH, TOK])
                    sp.dma_start(vb[:, m, :], src).then_inc(vb_loaded[m], 16)

            def store(t):
                sp.wait_ge(norm_ready[3], SUB * (t.n + 1))
                sp.dma_start(out_v[:, bass.ds(t.n, 1), :, :], y[t.par][:, :, :].unsqueeze(1)).then_inc(y_free[t.par], 16)

            sp.dma_start(s_att[:, :], att_w).then_inc(att_loaded, 16)
            load_xT(Tile(0, 0))
            sp.dma_start(s_con[:, :], consts).then_inc(con_loaded, 16)
            load_xT(Tile(0, 1))
            sp.dma_start(s_row[:, :, :], rows.unsqueeze(0).to_broadcast([P, 7, P])).then_inc(row_loaded, 16)
            load_xt(Tile(0, 0))
            sp.dma_start(s_wor[:, :, :], wo_rep).then_inc(y_free[0], 16)
            sp.dma_start(s_ffn[:, :], ffn_w).then_inc(y_free[1], 16)
            sp.dma_start(s_moe[:, :], moe_w).then_inc(moe_loaded, 16)
            sp.dma_start(s_gb[:, :], gate_row.to_broadcast([P, EXPERTS])).then_inc(gb_loaded, 16)

            def step(s):
                front, fetch, finish = s.plus(1), s.plus(2), s.plus(-2)
                if fetch.exists() and s.exists():
                    load_xT(fetch)
                if front.exists():
                    spread_vs(front)
                    if s.exists():
                        load_xt(front)
                if finish.exists():
                    store(finish)

            run_steps(sp, step)
            for i in range(2):
                sp.wait_ge(y_free[i], 16 * (TILES // 2 + 1))

        @block.tensor
        def _(pe):
            def project(t):
                pe.wait_ge(xT_loaded[t.par], 16 * (t.slot_uses + 1))
                wait(pe, qfac_ready, t.n)
                pe.matmul(pA[:, :], att("wq"), xT[t.par][:, :], start=True, stop=True).then_inc(q_proj, 1)
                wait(pe, vs_ready, t.n)
                pe.matmul(pB[:, :], att("wk"), xT[t.par][:, :], start=True, stop=True).then_inc(k_proj, 1)

            def project_v(t):
                pe.wait_ge(q_ready, t.n + 1)
                pe.matmul(pA[:, :], att("wv"), xT[t.par][:, :], start=True, stop=True).then_inc(v_proj, 1)

            def head_sums(t, dst, a, b, a_ready, b_ready, done):
                for i, (src, ready) in enumerate(((a, a_ready), (b, b_ready))):
                    pe.wait_ge(ready, t.n + 1)
                    for s in range(SUB):
                        at = i * HW + s * HEADS
                        mm = pe.matmul(dst[:, at:at + HEADS], src[:, s * P:(s + 1) * P], att("headsum"), start=True, stop=True)
                mm.then_inc(done, 1)

            def spread_T(dst, src, done):
                for s in range(SUB):
                    mm = pe.transpose(dst[:, s * P:(s + 1) * P], src[:, s * P:(s + 1) * P], ident)
                mm.then_inc(done, 1)

            def denominators_T(t):
                pe.wait_ge(rdenx_ready, 2 * t.n + 1)
                pe.wait_ge(v_ready, t.n + 1)
                spread_T(pA, rden_x[:, 0, :, :].rearrange("p a b -> p (a b)"), sinkT_ready)
                pe.wait_ge(rdenx_ready, 2 * t.n + 2)
                pe.wait_ge(k_ready, t.n + 1)
                spread_T(pB, rden_x[:, 1, :, :].rearrange("p a b -> p (a b)"), srcT_ready)

            def factor_T(t):
                pe.wait_ge(facx_ready, t.n + 1)
                pe.wait_ge(qsink_ready, t.n + 1)
                spread_T(pA, fac_x[:, :, :].rearrange("p a b -> p (a b)"), facT_ready)

            def cumulate_e(t):
                pe.wait_ge(esrc_ready, t.n + 1)
                pe.matmul(p_cume, upper, esrc[:, :], start=True, stop=False, skip_group_check=True)
                for lag in range(1, SUB):
                    mm = pe.matmul(p_cume[:, lag * HEADS:], ones, esrc[:, 0:(SUB - lag) * HEADS],
                                   start=False, stop=(lag == SUB - 1), skip_group_check=True)
                if t.par == 1:
                    pe.wait_ge(esum_ready, t.slot_uses + 1)
                    for s in range(SUB):
                        mm = pe.matmul(p_cume[:, s * HEADS:(s + 1) * HEADS], ones, esrc_sum[:, :], start=False,
                                       stop=True, skip_group_check=True)
                mm.then_inc(cume_ready, 1)

            def compensation_T(t):
                pe.wait_ge(compx_ready, t.n + 1)
                pe.wait_ge(ksrc_ready, t.n + 1)
                spread_T(pB, comp_x[:, :, :].rearrange("p a b -> p (a b)"), compT_ready)

            def reduce_out(t, m):
                pe.wait_ge(prod_ready, DH * t.n + m + 1)
                if m == 0:
                    wait(pe, res_ready[0], t.n)
                for s in range(SUB):
                    mm = pe.matmul(pO3[:, s, :], prod[:, m % 4, s * P:(s + 1) * P], s_wor[:, m, :],
                                   start=(m == 0 and s == 0), stop=(m == DH - 1), skip_group_check=True)
                mm.then_inc(red_ready, 1)

            def h_T(t):
                pe.wait_ge(norm_ready[0], SUB * (t.n + 1))
                wait(pe, udT_ready, t.n)
                for s in range(SUB):
                    mm = pe.transpose(pM[:, s * P:(s + 1) * P], n1[:, s, :], ident)
                mm.then_inc(hTp_ready, 1)

            def hidden(t, f):
                if f == 0:
                    pe.wait_ge(hT_ready, t.n + 1)
                if f >= 2:
                    pe.wait_ge(gelu_ready, FC * t.n + f - 1)
                pe.matmul(pG[f % 2][:, :], w1[:, f * P:(f + 1) * P], hT[:, :], start=True, stop=True).then_inc(w1_done, 1)

            def ffn_out(t, f):
                pe.wait_ge(gelu_ready, FC * t.n + f + 1)
                for s in range(SUB):
                    mm = pe.matmul(pY3[:, s, :], gel[:, f, s * P:(s + 1) * P], w2[:, f, :],
                                   start=(f == 0 and s == 0), stop=(f == FC - 1), skip_group_check=True)
                if f == FC - 1:
                    mm.then_inc(w2_done, 1)

            def x2_T(t):
                pe.wait_ge(norm_ready[2], SUB * (t.n + 1))
                pe.wait_ge(hT_ready, t.n + 1)
                for s in range(SUB):
                    mm = pe.transpose(pM[:, s * P:(s + 1) * P], x2[t.par][:, s, :], ident)
                mm.then_inc(x2Tp_ready, 1)

            def logits(t):
                pe.wait_ge(x2T_ready, t.n + 1)
                for s in range(SUB):
                    mm = pe.matmul(p_log[:, s, :], x2T[t.par][:, s * P:(s + 1) * P], moe("gate"), start=True, stop=True)
                mm.then_inc(logp_ready, 1)

            def lora_in(t):
                pe.wait_ge(gate_step, 17 * t.n + 1)
                for s in range(SUB):
                    mm = pe.matmul(pM3[:, s, :], x2T[t.par][:, s * P:(s + 1) * P], moe("la"), start=True, stop=True)
                mm.then_inc(up_ready, 1)

            def u_T(t, first_one):
                src, ready, done = (u1, u1_ready, u1Tp_ready) if first_one else (ud, ud_ready, udTp_ready)
                pe.wait_ge(ready, t.n + 1)
                if first_one:
                    pe.wait_ge(ud_ready, t.n + 1)
                else:
                    pe.wait_ge(u1T_ready, t.n + 1)
                for s in range(SUB):
                    mm = pe.transpose(pM[:, s * P:(s + 1) * P], src[:, s, :], ident)
                mm.then_inc(done, 1)

            def inter1(t, f):
                if f == 0:
                    pe.wait_ge(x2T_ready, t.n + 1)
                    pe.wait_ge(u1T_ready, t.n + 1)
                if f < 2:
                    if t.exists_next:
                        pe.wait_ge(gelu_ready, FC * (t.n + 1) + f + 3)
                    else:
                        pe.wait_ge(hsum_ready, FC * (t.n - 1) + f + 3)
                else:
                    pe.wait_ge(hsum_ready, FC * t.n + f - 1)
                pe.matmul(pG[f % 2][:, :], moe("wi")[:, f * P:(f + 1) * P], x2T[t.par][:, :], start=True, stop=False)
                pe.matmul(pG[f % 2][:, :], moe("lb")[:, f * P:(f + 1) * P], u1T[t.par][:, :], start=False, stop=True).then_inc(in1_done, 1)

            def inter2(t, f):
                if f == 0:
                    pe.wait_ge(udT_ready, t.n + 1)
                pe.wait_ge(relu_ready, FC * t.n + f + 1)
                pe.matmul(pG[f % 2][:, :], moe("lb")[:, f * P:(f + 1) * P], udT[t.par][:, :], start=False, stop=True,
                          skip_group_check=True).then_inc(in2_done, 1)

            def expert_out(t, f):
                pe.wait_ge(hsum_ready, FC * t.n + f + 1)
                if f == 0:
                    if t.exists_next:
                        pe.wait_ge(res_ready[1], t.n + 2)
                    else:
                        pe.wait_ge(res_ready[3], t.n)
                for s in range(SUB):
                    mm = pe.matmul(pY3[:, s, :], hsum[:, f, s * P:(s + 1) * P], wo[:, f, :],
                                   start=(f == 0 and s == 0), stop=(f == FC - 1), skip_group_check=True)
                mm.then_inc(wo_done, 1)

            pe.wait_ge(att_loaded, 16)
            pe.wait_ge(con_loaded, 16)
            project(Tile(0, 0))
            pe.wait_ge(moe_loaded, 16)
            pe.wait_ge(ones_ready, 2)
            for f in range(FC):
                mm = pe.matmul(pM[:, 0:P], bi_rep[:, f, :], wo[:, f, :], start=(f == 0), stop=(f == FC - 1))
            mm.then_inc(cmoe_mm, 1)

            def step(s):
                core, mlp, front, gate, exp = s, s.plus(-1), s.plus(1), s.plus(-1), s.plus(-2)
                exp.exists_next = exp.plus(1).exists()
                if isinstance(s.n, int) and s.n == 0:
                    pe.wait_ge(y_free[0], 16)
                if isinstance(s.n, int) and s.n == 1:
                    pe.wait_ge(y_free[1], 16)
                    pe.wait_ge(cmoe_ready, 1)
                for m in range(DH):
                    if core.exists():
                        reduce_out(core, m)
                    if mlp.exists():
                        if m == 2:
                            h_T(mlp)
                        if 3 <= m < 3 + FC:
                            hidden(mlp, m - 3)
                        if m >= 4:
                            ffn_out(mlp, m - 4)
                F, G, E = front.exists(), gate.exists(), exp.exists()
                if F and not (isinstance(front.n, int) and front.n == 0):
                    project(front)
                if E: inter1(exp, 0)
                if F: project_v(front)
                if E: inter2(exp, 0)
                if E: inter1(exp, 1)
                if F: head_sums(front, p_den, qk1, kq1, qk1_ready, kq1_ready, den_ready)
                if E: inter2(exp, 1); expert_out(exp, 0)
                if E: inter1(exp, 2)
                if F: denominators_T(front)
                if E: inter2(exp, 2); expert_out(exp, 1)
                if E: inter1(exp, 3)
                if G: x2_T(gate)
                if F: head_sums(front, p_cons, qk2, kq2, qk2_ready, kq2_ready, consp_ready)
                if E: inter2(exp, 3); expert_out(exp, 2)
                if F: cumulate_e(front); factor_T(front)
                if G: logits(gate)
                if F: compensation_T(front)
                if E: expert_out(exp, 3)
                if G: lora_in(gate); u_T(gate, True); u_T(gate, False)

            run_steps(pe, step)

        @block.scalar
        def _(act):
            def project_out(t):
                act.wait_ge(q_proj, t.n + 1)
                wait(act, kv_ready, DH * t.n)
                act.activation(q[:, :], pA[:, :], ACT.Sigmoid, bias=col("bq")).then_inc(q_ready, 1)
                act.wait_ge(k_proj, t.n + 1)
                act.activation(k[:, :], pB[:, :], ACT.Sigmoid, bias=col("bk")).then_inc(k_ready, 1)

            def v_out(t):
                act.wait_ge(v_proj, t.n + 1)
                act.activation(v[:, :], pA[:, :], ACT.Identity, bias=col("bv")).then_inc(v_ready, 1)

            def alloc_exp(t):
                act.wait_ge(cons_ready, t.n + 1)
                act.activation(tanh_half[:, :], cons[:, 0:HW], ACT.Tanh, scale=0.5).then_inc(tanh_ready, 1)
                act.wait_ge(clip_ready, t.n + 1)
                act.activation(esrc[:, :], clipped[:, :], ACT.Exp).then_inc(esrc_ready, 1)

            def normalise(t, i, src, dst):
                act.wait_ge(shift_ready[i], t.n + 1)
                for s in range(SUB):
                    act.activation(dst[:, s, :], src[:, s, :], ACT.Identity, bias=shift[i][:, s:s + 1],
                                   scale=rstd[i][:, s:s + 1]).then_inc(norm_ready[i], 1)

            def h_out(t):
                act.wait_ge(hTp_ready, t.n + 1)
                act.activation(hT[:, :], pM[:, :], ACT.Identity, bias=col("b1n"), scale=col("g1")).then_inc(hT_ready, 1)

            def gelu(t, f):
                act.wait_ge(w1_done, FC * t.n + f + 1)
                if f == 0:
                    wait(act, w2_done, t.n)
                act.activation(gel[:, f, :], pG[f % 2][:, :], ACT.Gelu, bias=col("b1", f)).then_inc(gelu_ready, 1)

            def x2T_out(t):
                act.wait_ge(x2Tp_ready, t.n + 1)
                act.activation(x2T[t.par][:, :], pM[:, :], ACT.Copy).then_inc(x2T_ready, 1)

            def gate_exp(t):
                act.wait_ge(gate_step, 17 * t.n + 3)
                act.activation(ex[:, :, :], prob[:, :, :], ACT.Exp).then_inc(ex_ready, 1)

            def uT_out(t):
                act.wait_ge(u1Tp_ready, t.n + 1)
                act.activation(u1T[t.par][:, :], pM[:, :], ACT.Copy).then_inc(u1T_ready, 1)
                act.wait_ge(udTp_ready, t.n + 1)
                act.activation(udT[t.par][:, :], pM[:, :], ACT.Copy).then_inc(udT_ready, 1)

            def relu(t, f):
                act.wait_ge(in1_done, FC * t.n + f + 1)
                act.activation(relu1[:, f % 2, :], pG[f % 2][:, :], ACT.Relu, bias=col("bi", f)).then_inc(relu_ready, 1)

            act.wait_ge(att_loaded, 16)

            def step(s):
                core, mlp, front, gate, exp = s, s.plus(-1), s.plus(1), s.plus(-1), s.plus(-2)
                if mlp.exists():
                    normalise(mlp, 0, res[0], n1)
                    h_out(mlp)
                    for f in range(FC):
                        gelu(mlp, f)
                F, G, E = front.exists(), gate.exists(), exp.exists()
                if F: project_out(front)
                if E: relu(exp, 0)
                if F: v_out(front)
                if E: relu(exp, 1)
                if G: normalise(gate, 1, res[1], n2)
                if E: relu(exp, 2)
                if E: relu(exp, 3)
                if G: normalise(gate, 2, res[2], x2[gate.par]); x2T_out(gate)
                if F: alloc_exp(front)
                if G: gate_exp(gate); uT_out(gate)
                if E:
                    act.wait_ge(y_free[exp.par], 16 * (exp.slot_uses + 1))
                    normalise(exp, 3, res[3], y[exp.par])

            run_steps(act, step)

        @block.gpsimd
        def _(pool):
            def inverse_std(t, i):
                pool.wait_ge(mv_ready[i], SUB * (t.n + 1))
                pool.tensor_tensor(var_eps[i][:, :], mv[i][:, :, 1], con("lneps"), ALU.add).then_inc(vareps_ready[i], 1)
                pool.wait_ge(vareps_ready[i], t.n + 1)
                pool.tensor_tensor(rstd[i][:, :], var_eps[i][:, :], con("mhalf"), ALU.pow).then_inc(rstd_ready[i], 1)

            def product(t, m):
                if m == 0:
                    pool.wait_ge(qfac_ready, t.n + 1)
                pool.wait_ge(cumkv_ready, DH * t.n + m + 1)
                wait(pool, red_ready, DH * t.n + m - 3)
                pool.tensor_tensor(prod[:, m % 4, :], cum_kv[t.par][:, m, :], q_fac[t.par][:, :], ALU.mult).then_inc(prod_ready, 1)

            def residuals(t):
                pool.wait_ge(xt_loaded[t.par], 16 * (t.slot_uses + 1))
                wait(pool, res_ready[0], t.n)
                pool.tensor_tensor(x_bo[:, :, :], xt[t.par][:, :, :], over_subs(row("bo")), ALU.add).then_inc(xbo_ready, 1)

            def shifted_x(t):
                wait(pool, res_ready[2], t.n)
                pool.tensor_tensor(x_b2n[:, :, :], xt[t.par][:, :, :], over_subs(row("b2n")), ALU.add).then_inc(xb2n_ready, 1)

            def h_residual(t):
                pool.wait_ge(norm_ready[0], SUB * (t.n + 1))
                wait(pool, res_ready[1], t.n)
                pool.tensor_tensor(h_res[:, :, :], n1[:, :, :], over_subs(row("g1")), ALU.mult).then_inc(hg_ready, 1)
                pool.wait_ge(hg_ready, t.n + 1)
                pool.tensor_tensor(h_res[:, :, :], h_res[:, :, :], over_subs(r_b1b2[:, :]), ALU.add).then_inc(hres_ready, 1)

            def outer_residual(t):
                pool.wait_ge(norm_ready[1], SUB * (t.n + 1))
                wait(pool, norm_ready[2], SUB * t.n)
                pool.tensor_tensor(res[2][:, :, :], n2[:, :, :], over_subs(row("g2")), ALU.mult).then_inc(zg_ready, 1)
                pool.wait_ge(zg_ready, t.n + 1)
                pool.wait_ge(xb2n_ready, t.n + 1)
                pool.tensor_tensor(res[2][:, :, :], res[2][:, :, :], x_b2n[:, :, :], ALU.add).then_inc(res_ready[2], 1)

            def gated_constant(t):
                pool.wait_ge(gsum_ready, t.n + 1)
                pool.wait_ge(norm_ready[2], SUB * (t.n + 1))
                pool.tensor_tensor(c_gate[:, :, :], over_subs(r_cmoe[:, :]),
                                   gate_sum[t.par][:, :].unsqueeze(2).to_broadcast([P, SUB, P]), ALU.mult).then_inc(cg_ready, 1)
                pool.wait_ge(cg_ready, t.n + 1)
                pool.tensor_tensor(x2c[t.par][:, :, :], x2[t.par][:, :, :], c_gate[:, :, :], ALU.add).then_inc(x2c_ready, 1)

            def compensation(t):
                pool.wait_ge(esrc_ready, t.n + 1)
                pool.tensor_tensor(e_norm[:, :], esrc[:, :], con("norm")[:, t.par * 2 * HW:t.par * 2 * HW + HW], ALU.mult).then_inc(enorm_ready, 1)
                pool.wait_ge(enorm_ready, t.n + 1)
                pool.wait_ge(rcume_ready, t.n + 1)
                pool.tensor_tensor(comp_x[:, :, :], e_norm[:, :].unsqueeze(2).to_broadcast([P, HW, DH]),
                                   rcum_e[:, :].unsqueeze(2).to_broadcast([P, HW, DH]), ALU.mult).then_inc(compx_ready, 1)

            pool.memset(onesrow[:, :], 1.0).then_inc(ones_ready, 1)
            pool.wait_ge(att_loaded, 16)
            pool.wait_ge(ones_ready, 1)
            bi_cols = s_att[:, W_ATT["cols"][0] + COLS["bi"]:W_ATT["cols"][0] + COLS["bi"] + FC]
            pool.tensor_tensor(bi_rep[:, :, :], onesrow[:, :].rearrange("p (f n) -> p f n", f=FC),
                               bi_cols.unsqueeze(2).to_broadcast([P, FC, P]), ALU.mult).then_inc(ones_ready, 1)
            pool.wait_ge(row_loaded, 16)
            pool.tensor_tensor(r_b1b2[:, :], row("b1n"), row("b2"), ALU.add).then_inc(rowsum_ready, 1)
            pool.wait_ge(rowsum_ready, 1)
            pool.wait_ge(con_loaded, 16)

            def step(s):
                core, mlp, front, gate, exp = s, s.plus(-1), s.plus(1), s.plus(-1), s.plus(-2)
                if mlp.exists():
                    inverse_std(mlp, 0)
                for m in range(DH):
                    if core.exists():
                        product(core, m)
                    if mlp.exists() and m == 3:
                        h_residual(mlp)
                if core.exists():
                    residuals(core)
                F, G, E = front.exists(), gate.exists(), exp.exists()
                if isinstance(s.n, int) and s.n == 1:
                    pool.wait_ge(cmoe_ready, 1)
                if G: shifted_x(gate); inverse_std(gate, 1); outer_residual(gate); inverse_std(gate, 2)
                if F: compensation(front)
                if G: gated_constant(gate)
                if E: inverse_std(exp, 3)

            run_steps(pool, step)

        @block.vector
        def _(dve):
            scan_ones = onesrow[:, :]

            def scan(dst, src, carry):
                return dve.tensor_tensor_scan(dst, scan_ones, src, carry, ALU.mult, ALU.add)

            def carry_of(t, bufs, start):
                return start if t.par == 0 else bufs[0][:, TOK - 1:TOK]

            def cumulate_qk(t):
                if t.par == 1:
                    dve.wait_ge(cumqs_ready, t.n)
                dve.wait_ge(q_ready, t.n + 1)
                scan(cum_q[t.par][:, :], q[:, :], carry_of(t, cum_q, ATT_EPS)).then_inc(cumq_ready, 1)
                dve.wait_ge(k_ready, t.n + 1)
                scan(cum_k[t.par][:, :], k[:, :], carry_of(t, cum_k, ATT_EPS)).then_inc(cumk_ready, 1)

            def pair_products(t, cq, ck, kq, qk, cq_ready, ck_ready, kq_ready, qk_ready):
                dve.wait_ge(cq_ready, t.n + 1)
                dve.scalar_tensor_tensor(kq[:, :], k[:, :], ATT_EPS, cq[t.par][:, :], ALU.add, ALU.mult).then_inc(kq_ready, 1)
                dve.wait_ge(ck_ready, t.n + 1)
                dve.scalar_tensor_tensor(qk[:, :], q[:, :], ATT_EPS, ck[t.par][:, :], ALU.add, ALU.mult).then_inc(qk_ready, 1)

            def inverse_denominators(t):
                dve.wait_ge(den_ready, t.n + 1)
                dve.reciprocal(rden[:, :], p_den).then_inc(rden_ready, 1)
                dve.wait_ge(rden_ready, t.n + 1)
                nrm = con("norm")[:, t.par * 2 * HW:t.par * 2 * HW + HW]
                for i in range(2):
                    dve.tensor_tensor(rden_x[:, i, :, :], rden[:, i * HW:(i + 1) * HW].unsqueeze(2).to_broadcast([P, HW, DH]),
                                      nrm.unsqueeze(2).to_broadcast([P, HW, DH]), ALU.mult).then_inc(rdenx_ready, 1)

            def sink_source(t):
                dve.wait_ge(sinkT_ready, t.n + 1)
                dve.tensor_tensor(q_sink[:, :], q[:, :], pA[:, :], ALU.mult).then_inc(qsink_ready, 1)
                dve.wait_ge(srcT_ready, t.n + 1)
                dve.tensor_tensor(k_src[:, :], k[:, :], pB[:, :], ALU.mult).then_inc(ksrc_ready, 1)

            def cumulate_sink_source(t):
                dve.wait_ge(qsink_ready, t.n + 1)
                scan(cum_qs[t.par][:, :], q_sink[:, :], carry_of(t, cum_qs, ATT_EPS)).then_inc(cumqs_ready, 1)
                dve.wait_ge(ksrc_ready, t.n + 1)
                scan(cum_ks[t.par][:, :], k_src[:, :], carry_of(t, cum_ks, ATT_EPS)).then_inc(cumks_ready, 1)

            def conserved(t):
                dve.wait_ge(consp_ready, t.n + 1)
                at = t.par * 2 * HW
                dve.tensor_tensor(cons[:, :], p_cons, con("inorm")[:, at:at + 2 * HW], ALU.mult).then_inc(cons_ready, 1)
                dve.wait_ge(cons_ready, t.n + 1)
                dve.tensor_scalar(clipped[:, :], cons[:, HW:2 * HW], -1.0, 1.0, ALU.max, ALU.min).then_inc(clip_ready, 1)

            def allocation(t):
                dve.wait_ge(tanh_ready, t.n + 1)
                dve.tensor_scalar(alloc[:, :], tanh_half[:, :], 0.5, 0.5, ALU.mult, ALU.add).then_inc(alloc_ready, 1)
                dve.wait_ge(alloc_ready, t.n + 1)
                dve.tensor_tensor(fac_x[:, :, :], rden[:, 0:HW].unsqueeze(2).to_broadcast([P, HW, DH]),
                                  alloc[:, :].unsqueeze(2).to_broadcast([P, HW, DH]), ALU.mult).then_inc(facx_ready, 1)
                if t.par == 0:
                    dve.wait_ge(esrc_ready, t.n + 1)
                    dve.tensor_reduce(esrc_sum[:, :], esrc[:, :].rearrange("p (s h) -> p h s", s=SUB), AX_X, ALU.add).then_inc(esum_ready, 1)

            def inverse_cum_e(t):
                dve.wait_ge(cume_ready, t.n + 1)
                dve.reciprocal(rcum_e[:, :], p_cume).then_inc(rcume_ready, 1)

            def query_factor(t):
                dve.wait_ge(facT_ready, t.n + 1)
                wait(dve, prod_ready, DH * (t.n - 1))
                dve.tensor_tensor(q_fac[t.par][:, :], q[:, :], pA[:, :], ALU.mult).then_inc(qfac_ready, 1)

            def values(t):
                dve.wait_ge(compT_ready, t.n + 1)
                dve.tensor_tensor(vs[:, :], v[:, :], pB[:, :], ALU.mult).then_inc(vs_ready, 1)

            def outer_product(t, m):
                dve.wait_ge(vb_loaded[m], 16 * (t.n + 1))
                wait(dve, cumkv_ready, DH * t.n + m - 2)
                dve.tensor_tensor(kv[:, m % 3, :], k[:, :], vb[:, m, :], ALU.mult).then_inc(kv_ready, 1)

            def cumulate_kv(t, m):
                dve.wait_ge(kv_ready, DH * t.n + m + 1)
                start = 0.0 if t.par == 0 else cum_kv[0][:, m, TOK - 1:TOK]
                dve.tensor_tensor_scan(cum_kv[t.par][:, m, :], scan_ones, kv[:, m % 3, :], start, ALU.mult, ALU.add).then_inc(cumkv_ready, 1)

            def moments(t, i):
                dve.wait_ge(res_ready[i], t.n + 1)
                for s in range(SUB):
                    dve.bn_stats(stats[i][:, s, :], res[i][:, s, :]).then_inc(stats_ready[i], 1)
                dve.wait_ge(stats_ready[i], SUB * (t.n + 1))
                dve.memset(fence[:, :], 0.0)
                for s in range(SUB):
                    dve.bn_aggr(mv[i][:, s, :], stats[i][:, s, :]).then_inc(mv_ready[i], 1)

            def shifts(t, i):
                dve.wait_ge(rstd_ready[i], t.n + 1)
                dve.scalar_tensor_tensor(shift[i][:, :], mv[i][:, :, 0], -1.0, rstd[i][:, :], ALU.mult, ALU.mult).then_inc(shift_ready[i], 1)

            def attention_residual(t):
                dve.wait_ge(red_ready, DH * (t.n + 1))
                dve.wait_ge(xbo_ready, t.n + 1)
                dve.tensor_tensor(res[0][:, :, :], x_bo[:, :, :], pO3, ALU.add).then_inc(res_ready[0], 1)

            def ffn_residual(t):
                dve.wait_ge(w2_done, t.n + 1)
                dve.wait_ge(hres_ready, t.n + 1)
                dve.tensor_tensor(res[1][:, :, :], h_res[:, :, :], pY3, ALU.add).then_inc(res_ready[1], 1)

            def bc(a):
                return a.unsqueeze(2).to_broadcast([P, SUB, EXPERTS])

            def gate_chain(t, part):
                prefer = con("prefer").rearrange("p (s e) -> p s e", s=SUB)
                done = [17 * t.n + (0, 3, 6)[part]]

                def link(ins):
                    ins.then_inc(gate_step, 1)
                    done[0] = done[0] + 1
                    dve.wait_ge(gate_step, done[0])

                if part == 0:
                    dve.wait_ge(logp_ready, t.n + 1)
                    link(dve.tensor_tensor(logit[:, :, :], p_log, s_gb[:, :].unsqueeze(1).to_broadcast([P, SUB, EXPERTS]), ALU.add))
                    link(dve.tensor_reduce(m_log[:, :], logit[:, :, :], AX_X, ALU.max))
                    link(dve.tensor_tensor(prob[:, :, :], logit[:, :, :], bc(m_log[:, :]), ALU.subtract))
                if part == 1:
                    dve.wait_ge(ex_ready, t.n + 1)
                    link(dve.tensor_reduce(s_ex[:, :], ex[:, :, :], AX_X, ALU.add))
                    link(dve.reciprocal(r_ex[:, :], s_ex[:, :]))
                    link(dve.tensor_tensor(prob[:, :, :], ex[:, :, :], bc(r_ex[:, :]), ALU.mult))
                if part == 2:
                    link(dve.tensor_reduce(top1[:, :], prob[:, :, :], AX_X, ALU.max))
                    link(dve.tensor_tensor(eq[:, :, :], prob[:, :, :], bc(top1[:, :]), ALU.is_equal))
                    link(dve.tensor_tensor(pick[:, :, :], eq[:, :, :], prefer, ALU.mult))
                    link(dve.tensor_reduce(m_pick[:, :], pick[:, :, :], AX_X, ALU.max))
                    link(dve.tensor_tensor(first[:, :, :], pick[:, :, :], bc(m_pick[:, :]), ALU.is_equal))
                    link(dve.scalar_tensor_tensor(prob2[:, :, :], first[:, :, :], -2.0, prob[:, :, :], ALU.mult, ALU.add))
                    link(dve.tensor_reduce(top2[:, :], prob2[:, :, :], AX_X, ALU.max))
                    link(dve.tensor_tensor(eq[:, :, :], prob2[:, :, :], bc(top2[:, :]), ALU.is_equal))
                    link(dve.tensor_tensor(pick[:, :, :], eq[:, :, :], prefer, ALU.mult))
                    link(dve.tensor_reduce(m_pick[:, :], pick[:, :, :], AX_X, ALU.max))
                    dve.tensor_tensor(gate_sum[t.par][:, :], top1[:, :], top2[:, :], ALU.add).then_inc(gsum_ready, 1)
                    dve.tensor_tensor(second[:, :, :], pick[:, :, :], bc(m_pick[:, :]), ALU.is_equal).then_inc(gate_step, 1)

            def masked_lora(t):
                dve.wait_ge(gate_step, 17 * (t.n + 1))
                dve.tensor_tensor(delta[:, :, :], second[:, :, :], first[:, :, :], ALU.subtract).then_inc(delta_ready, 1)
                dve.wait_ge(up_ready, t.n + 1)
                u = pM[:, :].rearrange("p (a r) -> p a r", r=RANK)
                for dst, mask, ready in ((u1, first, u1_ready), (ud, delta, ud_ready)):
                    if mask is delta:
                        dve.wait_ge(delta_ready, t.n + 1)
                    dve.tensor_tensor(dst[:, :, :].rearrange("p s (e r) -> p (s e) r", r=RANK),
                                      mask[:, :, :].rearrange("p s e -> p (s e)").unsqueeze(2).to_broadcast([P, SUB * EXPERTS, RANK]),
                                      u, ALU.mult).then_inc(ready, 1)

            def second_relu(t, f):
                dve.wait_ge(in2_done, FC * t.n + f + 1)
                if f == 0:
                    if t.plus(1).exists():
                        dve.wait_ge(w2_done, t.n + 2)
                    else:
                        dve.wait_ge(wo_done, FC * t.n)
                dve.scalar_tensor_tensor(hsum[:, f, :], pG[f % 2][:, :], neg_bi[:, f:f + 1], relu1[:, f % 2, :],
                                         ALU.max, ALU.add).then_inc(hsum_ready, 1)

            def expert_residual(t):
                dve.wait_ge(wo_done, FC * (t.n + 1))
                dve.wait_ge(x2c_ready, t.n + 1)
                for s in range(SUB):
                    ins = dve.scalar_tensor_tensor(res[3][:, s, :], pY3[:, s, :], gate_sum[t.par][:, s:s + 1],
                                                   x2c[t.par][:, s, :], ALU.mult, ALU.add)
                ins.then_inc(res_ready[3], 1)

            dve.wait_ge(att_loaded, 16)
            bi_cols = s_att[:, W_ATT["cols"][0] + COLS["bi"]:W_ATT["cols"][0] + COLS["bi"] + FC]
            dve.tensor_scalar(neg_bi[:, :], bi_cols, -1.0, None, ALU.mult).then_inc(negbi_ready, 1)
            dve.wait_ge(negbi_ready, 1)
            dve.wait_ge(ones_ready, 1)
            dve.wait_ge(con_loaded, 16)
            dve.wait_ge(gb_loaded, 16)
            dve.wait_ge(row_loaded, 16)

            def step(s):
                core, mlp, front, gate, exp = s, s.plus(-1), s.plus(1), s.plus(-1), s.plus(-2)
                if isinstance(s.n, int) and s.n == 0:
                    dve.wait_ge(cmoe_mm, 1)
                    dve.scalar_tensor_tensor(r_cmoe[:, :], row("bffn"), 2.0, pM[:, 0:P], ALU.mult, ALU.add).then_inc(cmoe_ready, 1)
                if mlp.exists():
                    attention_residual(mlp)
                for m in range(DH + 1):
                    if core.exists():
                        if m < DH:
                            outer_product(core, m)
                        if m >= 1:
                            cumulate_kv(core, m - 1)
                    if mlp.exists():
                        if m == 0:
                            moments(mlp, 0)
                        if m == 2:
                            shifts(mlp, 0)
                F, G, E = front.exists(), gate.exists(), exp.exists()
                if G: ffn_residual(gate)
                if F: cumulate_qk(front)
                if G: moments(gate, 1)
                if F: pair_products(front, cum_q, cum_k, kq1, qk1, cumq_ready, cumk_ready, kq1_ready, qk1_ready)
                if E: second_relu(exp, 0)
                if G: shifts(gate, 1)
                if F: inverse_denominators(front)
                if E: second_relu(exp, 1)
                if F: sink_source(front)
                if E: second_relu(exp, 2)
                if F: cumulate_sink_source(front)
                if G: moments(gate, 2)
                if F: pair_products(front, cum_qs, cum_ks, kq2, qk2, cumqs_ready, cumks_ready, kq2_ready, qk2_ready)
                if G: shifts(gate, 2)
                if F: conserved(front)
                if E: second_relu(exp, 3)
                if F: allocation(front); inverse_cum_e(front); query_factor(front)
                if G: gate_chain(gate, 0)
                if F: values(front)
                if G: gate_chain(gate, 1); gate_chain(gate, 2); masked_lora(gate)
                if E: expert_residual(exp); moments(exp, 3); shifts(exp, 3)

            run_steps(dve, step)


_OUTS = [((BATCH, LENGTH, P), "float32")]


def kernel(**inputs):
    import numpy as np
    import concourse.bacc as bacc
    from concourse.bass_utils import run_bass_kernel_spmd

    a = {n[len("L0_attn_"):]: np.asarray(v) for n, v in inputs.items() if n.startswith("L0_attn_")}
    m = {n[len("L0_ffn_"):]: np.asarray(v) for n, v in inputs.items() if n.startswith("L0_ffn_")}

    def col(v):
        return v.reshape(-1, P).T

    x = a["inputs"].reshape(BATCH * LENGTH, P)
    headsum = np.kron(np.eye(HEADS), np.ones((DH, 1))).astype(np.float32)
    att_w = np.concatenate([a["Wq"], a["Wk"], a["Wv"], headsum, col(a["bq"]), col(a["bk"]), col(a["bv"]),
                            col(a["ln1_g"]), col(a["ln1_b"]), col(a["b1"]), col(m["bi"]), col(a["bq"])[:, 0:1], col(a["bq"])[:, 0:1]], axis=1)
    token = (TOK * np.arange(2)[None, :, None, None, None] + P * np.arange(SUB)[None, None, None, :, None]
             + np.arange(P)[:, None, None, None, None] + 1 + 0 * np.arange(2)[None, None, :, None, None]
             + 0 * np.arange(HEADS)[None, None, None, None, :]).astype(np.float32)
    norm = token.reshape(P, 4 * HW)
    prefer = np.tile(np.arange(EXPERTS, 0, -1), (P, SUB)).astype(np.float32)
    consts = np.concatenate([np.eye(P), np.triu(np.ones((P, P))), np.ones((P, P)), norm, 1.0 / norm, prefer,
                             np.full((P, SUB), -0.5), np.full((P, SUB), LN_EPS)], axis=1).astype(np.float32)
    wo_rep = np.repeat(a["Wo"].reshape(HEADS, 1, DH, P), DH, axis=1).reshape(P, DH, P)
    rows = np.stack([a["bo"], a["ln1_g"], a["ln1_b"], a["b2"], a["ln2_g"], a["ln2_b"], m["bo"]])
    gate_row = m["gate_b"].reshape(1, EXPERTS)

    def pieces(w):
        return w.reshape(FC, P, P).transpose(1, 0, 2).reshape(P, FF)

    ffn_w = np.concatenate([a["W1"], pieces(a["W2"])], axis=1)
    moe_w = np.concatenate([m["lora_A"].reshape(P, P).T, m["gate_w"].T, m["wi"].T,
                            m["lora_B"].transpose(0, 2, 1).reshape(P, FF), pieces(m["wo"].T)], axis=1)
    arrays = {"x": x, "x_t": x.T, "att_w": att_w, "consts": consts, "wo_rep": wo_rep, "rows": rows,
              "gate_row": gate_row, "ffn_w": ffn_w, "moe_w": moe_w}
    arrays = {n: np.ascontiguousarray(v) for n, v in arrays.items()}
    nc = bacc.Bacc("TRN2", target_bir_lowering=False, num_devices=1)
    args = [nc.dram_tensor(n, v.shape, F32, kind="ExternalInput").ap() for n, v in arrays.items()]
    out = nc.dram_tensor("out", (BATCH * LENGTH, P), F32, kind="ExternalOutput").ap()
    build(nc, *args, out)
    r = run_bass_kernel_spmd(nc, [arrays], core_ids=[0])
    return r.results[0]["out"].reshape(BATCH, LENGTH, P)
```

```python
import concourse.bass as bass
from concourse import mybir
from contextlib import ExitStack

F32 = mybir.dt.float32
ALU = mybir.AluOpType
ACT = mybir.ActivationFunctionType
AX_X = mybir.AxisListType.X

P = 128
BATCH, LENGTH = 4, 1024
HEADS, DH = 16, 8
FF = 512
EXPERTS, RANK = 8, 16
TOK = 512
SUB = TOK // P
TILES = BATCH * LENGTH // TOK
FC = FF // P
ATT_EPS = 1e-6
LN_EPS = 1e-5
GATE_STEPS = 18
HW = SUB * HEADS

W_ATT = {"wq": (0, 128), "wk": (128, 256), "wv": (256, 384), "headsum": (384, 400), "cols": (400, 415)}
COLS = {"bq": 0, "bk": 1, "bv": 2, "g1": 3, "b1n": 4, "b1": 5, "bi": 9}
N_COLS = 15
W_CONST = {"ident": (0, 128), "upper": (128, 256), "ones": (256, 384), "norm": (384, 640), "inorm": (640, 896),
           "prefer": (896, 928), "mhalf": (928, 932), "lneps": (932, 936)}
ROWS = {"bo": 0, "g1": 1, "b1n": 2, "b2": 3, "g2": 4, "b2n": 5, "bffn": 6}
W_FFN = {"w1": (0, 512), "w2": (512, 1024)}
W_MOE = {"la": (0, 128), "gate": (128, 136), "wi": (136, 648), "lb": (648, 1160), "wo": (1160, 1672)}


class Tile:

    def __init__(self, pair, c):
        self.pair, self.c = pair, c
        self.n = 2 * pair + c
        self.par = c % 2
        self.slot_uses = pair + c // 2

    def plus(self, k):
        return Tile(self.pair, self.c + k)

    def exists(self):
        return not isinstance(self.n, int) or 0 <= self.n < TILES


def wait(eng, sem, value):
    if isinstance(value, int) and value <= 0:
        return
    eng.wait_ge(sem, value)


def run_steps(eng, step):
    for c in (-1, 0, 1, 2):
        step(Tile(0, c))
    with eng.Fori(1, 3) as pair:
        step(Tile(pair, 1))
        step(Tile(pair, 2))
    for c in (1, 2, 3):
        step(Tile(3, c))


def build(nc, x, x_t, att_w, consts, wo_rep, rows, gate_row, ffn_w, moe_w, out):
    ctx = ExitStack()
    with ctx:
        def sb(name, shape):
            return ctx.enter_context(nc.sbuf_tensor(name, shape, F32))

        def bank(name):
            return ctx.enter_context(nc.psum_tensor(name, [P, TOK], F32))

        def sem(name):
            return ctx.enter_context(nc.semaphore(name))

        s_att = sb("s_att", [P, 415])
        s_con = sb("s_con", [P, 936])
        s_wor = sb("s_wor", [P, DH, P])
        s_row = sb("s_row", [P, 7, P])
        s_gb = sb("s_gb", [P, EXPERTS])
        s_ffn = sb("s_ffn", [P, 2 * FF])
        s_moe = sb("s_moe", [P, 1672])

        def att(name):
            return s_att[:, slice(*W_ATT[name])]

        def col(name, k=0):
            at = W_ATT["cols"][0] + COLS[name] + k
            return s_att[:, at:at + 1]

        def con(name):
            return s_con[:, slice(*W_CONST[name])]

        def moe(name):
            return s_moe[:, slice(*W_MOE[name])]

        def row(name):
            return s_row[:, ROWS[name], :]

        def over_subs(r):
            return r.unsqueeze(1).to_broadcast([P, SUB, P])

        w1 = s_ffn[:, 0:512]
        w2 = s_ffn[:, 512:1024].rearrange("p (f n) -> p f n", f=FC)
        wo = moe("wo").rearrange("p (f n) -> p f n", f=FC)
        ident, upper, ones = con("ident"), con("upper"), con("ones")

        neg_bi = sb("neg_bi", [P, FC])
        r_b1b2 = sb("r_b1b2", [P, P])
        r_cmoe = sb("r_cmoe", [P, P])
        bi_rep = sb("bi_rep", [P, FC, P])
        onesrow = sb("onesrow", [P, TOK])

        xT = [sb(f"xT{i}", [P, TOK]) for i in range(2)]
        xt = [sb(f"xt{i}", [P, SUB, P]) for i in range(2)]
        q = [sb(f"q{i}", [P, TOK]) for i in range(2)]
        k = [sb(f"k{i}", [P, TOK]) for i in range(2)]
        v = sb("v", [P, TOK])
        cum_k = [sb(f"cum_k{i}", [P, TOK]) for i in range(2)]
        cum_q = [sb(f"cum_q{i}", [P, TOK]) for i in range(2)]
        cum_ks = [sb(f"cum_ks{i}", [P, TOK]) for i in range(2)]
        cum_qs = [sb(f"cum_qs{i}", [P, TOK]) for i in range(2)]
        qk, kq = sb("qk", [P, TOK]), sb("kq", [P, TOK])
        k_src, q_sink = sb("k_src", [P, TOK]), sb("q_sink", [P, TOK])
        rden = sb("rden", [P, 2 * HW])
        rden_n = sb("rden_n", [P, 2 * HW])
        rden_x = sb("rden_x", [P, 2, HW, DH])
        cons = sb("cons", [P, 2 * HW])
        clipped = sb("clipped", [P, HW])
        tanh_half = sb("tanh_half", [P, HW])
        alloc = sb("alloc", [P, HW])
        fac_x = rden_x[:, 0, :, :]
        esrc = sb("esrc", [P, HW])
        esrc_sum = sb("esrc_sum", [P, HEADS])
        rcum_e, e_norm = sb("rcum_e", [P, HW]), sb("e_norm", [P, HW])
        comp_x = rden_x[:, 1, :, :]
        q_fac = [sb(f"q_fac{i}", [P, TOK]) for i in range(2)]
        vs = sb("vs", [P, TOK])
        vb = sb("vb", [P, DH, TOK])
        kv = sb("kv", [P, 3, TOK])
        cum_kv = [sb(f"cum_kv{i}", [P, DH, TOK]) for i in range(2)]
        prod = sb("prod", [P, 4, TOK])

        x_bo = sb("x_bo", [P, SUB, P])
        x_b2n = sb("x_b2n", [P, SUB, P])
        res = [sb(f"res{i}", [P, SUB, P]) for i in range(4)]
        stats = [sb(f"stats{i}", [P, SUB, 6]) for i in range(4)]
        mv = [sb(f"mv{i}", [P, SUB, 2]) for i in range(4)]
        var_eps = [sb(f"var_eps{i}", [P, SUB]) for i in range(4)]
        rstd = [sb(f"rstd{i}", [P, SUB]) for i in range(4)]
        shift3 = sb("shift3", [P, SUB])
        fence = sb("fence", [P, 1])
        n1, n2 = sb("n1", [P, SUB, P]), sb("n2", [P, SUB, P])
        x2 = sb("x2", [P, SUB, P])
        y = [sb(f"y{i}", [P, SUB, P]) for i in range(2)]
        hT = sb("hT", [P, TOK])
        h_res = sb("h_res", [P, SUB, P])
        gel = sb("gel", [P, FC, TOK])
        hsum = gel

        x2T = [sb(f"x2T{i}", [P, TOK]) for i in range(2)]
        logit, prob, ex = (sb(n, [P, SUB, EXPERTS]) for n in ("logit", "prob", "ex"))
        prob2, eq, pick = (sb(n, [P, SUB, EXPERTS]) for n in ("prob2", "eq", "pick"))
        first, second, delta = (sb(n, [P, SUB, EXPERTS]) for n in ("first", "second", "delta"))
        m_log, s_ex, r_ex, top1, top2, m_pick = (sb(n, [P, SUB]) for n in ("m_log", "s_ex", "r_ex", "top1", "top2", "m_pick"))
        gate_sum = sb("gate_sum", [P, SUB])
        u1, ud = sb("u1", [P, SUB, P]), sb("ud", [P, SUB, P])
        u1T = sb("u1T", [P, TOK])
        udT = sb("udT", [P, TOK])
        c_gate = sb("c_gate", [P, SUB, P])
        x2c = sb("x2c", [P, SUB, P])
        relu1 = sb("relu1", [P, 2, TOK])

        pA, pB, pS, pO = bank("pA"), bank("pB"), bank("pS"), bank("pO")
        pG = [bank("pG0"), bank("pG1")]
        pY, pM = bank("pY"), bank("pM")
        pO3, pY3, pM3 = (b[:, :].rearrange("p (s n) -> p s n", s=SUB) for b in (pO, pY, pM))
        p_den, p_cons, p_cume = pS[:, 0:2 * HW], pS[:, 2 * HW:4 * HW], pS[:, 4 * HW:5 * HW]
        p_log = pM[:, 0:SUB * EXPERTS].rearrange("p (s e) -> p s e", s=SUB)

        att_loaded, con_loaded = sem("att_loaded"), sem("con_loaded")
        row_loaded, gb_loaded = sem("row_loaded"), sem("gb_loaded")
        moe_loaded = sem("moe_loaded")
        xT_loaded = [sem(f"xT_loaded{i}") for i in range(2)]
        xt_loaded = [sem(f"xt_loaded{i}") for i in range(2)]
        vb_loaded = [sem(f"vb_loaded{m}") for m in range(DH)]
        y_free = [sem(f"y_free{i}") for i in range(2)]
        ones_ready, negbi_ready, rowsum_ready, cmoe_mm, cmoe_ready = (
            sem(n) for n in ("ones_ready", "negbi_ready", "rowsum_ready", "cmoe_mm", "cmoe_ready"))
        q_proj, k_proj, v_proj = sem("q_proj"), sem("k_proj"), sem("v_proj")
        q_ready, k_ready, v_ready = sem("q_ready"), sem("k_ready"), sem("v_ready")
        cumk_ready, cumq_ready = sem("cumk_ready"), sem("cumq_ready")
        qk1_ready, kq1_ready, den_ready = sem("qk1_ready"), sem("kq1_ready"), sem("den_ready")
        rden_ready, rdenn_ready, rdenx_ready = sem("rden_ready"), sem("rdenn_ready"), sem("rdenx_ready")
        sinkT_ready, srcT_ready = sem("sinkT_ready"), sem("srcT_ready")
        qsink_ready, ksrc_ready = sem("qsink_ready"), sem("ksrc_ready")
        cumks_ready, cumqs_ready = sem("cumks_ready"), sem("cumqs_ready")
        qk2_ready, kq2_ready, consp_ready = sem("qk2_ready"), sem("kq2_ready"), sem("consp_ready")
        cons_ready, clip_ready, tanh_ready, esrc_ready = (sem(n) for n in ("cons_ready", "clip_ready", "tanh_ready", "esrc_ready"))
        alloc_ready, facx_ready, facT_ready, qfac_ready = (sem(n) for n in ("alloc_ready", "facx_ready", "facT_ready", "qfac_ready"))
        cume_ready, rcume_ready, enorm_ready, compx_ready = (sem(n) for n in ("cume_ready", "rcume_ready", "enorm_ready", "compx_ready"))
        esum_ready = sem("esum_ready")
        compT_ready, vs_ready = sem("compT_ready"), sem("vs_ready")
        kv_ready, cumkv_ready, prod_ready, red_ready = (sem(n) for n in ("kv_ready", "cumkv_ready", "prod_ready", "red_ready"))
        res_ready = [sem(f"res_ready{i}") for i in range(4)]
        stats_ready = [sem(f"stats_ready{i}") for i in range(4)]
        mv_ready = [sem(f"mv_ready{i}") for i in range(4)]
        vareps_ready = [sem(f"vareps_ready{i}") for i in range(4)]
        rstd_ready = [sem(f"rstd_ready{i}") for i in range(4)]
        shift3_ready = sem("shift3_ready")
        norm_ready = [sem(f"norm_ready{i}") for i in range(4)]
        xbo_ready, xb2n_ready = sem("xbo_ready"), sem("xb2n_ready")
        hTp_ready, hT_ready, hg_ready, hres_ready = (sem(n) for n in ("hTp_ready", "hT_ready", "hg_ready", "hres_ready"))
        w1_done, gelu_ready, w2_done = sem("w1_done"), sem("gelu_ready"), sem("w2_done")
        zg_ready = sem("zg_ready")
        x2Tp_ready, x2T_ready, logp_ready, up_ready = (sem(n) for n in ("x2Tp_ready", "x2T_ready", "logp_ready", "up_ready"))
        gate_step = sem("gate_step")
        ex_ready = sem("ex_ready")
        gsum_ready = sem("gsum_ready")
        u1_ready, ud_ready, u1Tp_ready, udTp_ready, u1T_ready, udT_ready = (
            sem(n) for n in ("u1_ready", "ud_ready", "u1Tp_ready", "udTp_ready", "u1T_ready", "udT_ready"))
        cg_ready, x2c_ready = sem("cg_ready"), sem("x2c_ready")
        in1_done, relu_ready, in2_done, hsum_ready, wo_done = (
            sem(n) for n in ("in1_done", "relu_ready", "in2_done", "hsum_ready", "wo_done"))

        x_v = x.rearrange("(t s p) d -> p t s d", s=SUB, p=P)
        out_v = out.rearrange("(t s p) d -> p t s d", s=SUB, p=P)

        block = ctx.enter_context(nc.Block())

        @block.sync
        def _(sp):
            def load_xT(t):
                wait(sp, v_proj, t.n - 1)
                sp.dma_start(xT[t.par][:, :], x_t[:, bass.ds(t.n * TOK, TOK)]).then_inc(xT_loaded[t.par], 16)

            def load_xt(t):
                wait(sp, xbo_ready, t.n - 1)
                wait(sp, xb2n_ready, t.n - 1)
                sp.dma_start(xt[t.par][:, :, :].unsqueeze(1), x_v[:, bass.ds(t.n, 1), :, :]).then_inc(xt_loaded[t.par], 16)

            def spread_vs(t, m):
                sp.wait_ge(vs_ready, t.n + 1)
                src = vs[m:P:DH, :].unsqueeze(1).to_broadcast([HEADS, DH, TOK])
                sp.dma_start(vb[:, m, :], src).then_inc(vb_loaded[m], 16)

            def store(t):
                sp.wait_ge(norm_ready[3], SUB * (t.n + 1))
                sp.dma_start(out_v[:, bass.ds(t.n, 1), :, :], y[t.par][:, :, :].unsqueeze(1)).then_inc(y_free[t.par], 16)

            sp.dma_start(s_att[:, :], att_w).then_inc(att_loaded, 16)
            load_xT(Tile(0, 0))
            sp.dma_start(s_con[:, :], consts).then_inc(con_loaded, 16)
            load_xT(Tile(0, 1))
            sp.dma_start(s_row[:, :, :], rows.unsqueeze(0).to_broadcast([P, 7, P])).then_inc(row_loaded, 16)
            load_xt(Tile(0, 0))
            sp.dma_start(s_wor[:, :, :], wo_rep).then_inc(y_free[0], 16)
            sp.dma_start(s_ffn[:, :], ffn_w).then_inc(y_free[1], 16)
            sp.dma_start(s_moe[:, :], moe_w).then_inc(moe_loaded, 16)
            sp.dma_start(s_gb[:, :], gate_row.to_broadcast([P, EXPERTS])).then_inc(gb_loaded, 16)

            def step(s):
                a, b, c, d = s.plus(1), s, s.plus(-1), s.plus(-2)
                A, B, C, D = a.exists(), b.exists(), c.exists(), d.exists()
                if A and not (isinstance(a.n, int) and a.n < 2): load_xT(a)
                if B: spread_vs(b, 3); spread_vs(b, 4); spread_vs(b, 5); spread_vs(b, 6)
                if A and not (isinstance(a.n, int) and a.n < 1): load_xt(a)
                if B: spread_vs(b, 7)
                if A: spread_vs(a, 0); spread_vs(a, 1)
                if D: store(d)
                if A: spread_vs(a, 2)
            run_steps(sp, step)
            for i in range(2):
                sp.wait_ge(y_free[i], 16 * (TILES // 2 + 1))

        @block.tensor
        def _(pe):
            def project_q(t):
                pe.wait_ge(xT_loaded[t.par], 16 * (t.slot_uses + 1))
                wait(pe, qfac_ready, t.n)
                pe.matmul(pA[:, :], att("wq"), xT[t.par][:, :], start=True, stop=True).then_inc(q_proj, 1)

            def project_k(t):
                pe.wait_ge(xT_loaded[t.par], 16 * (t.slot_uses + 1))
                wait(pe, vs_ready, t.n)
                pe.matmul(pB[:, :], att("wk"), xT[t.par][:, :], start=True, stop=True).then_inc(k_proj, 1)

            def project_v(t):
                pe.wait_ge(q_ready, t.n + 1)
                pe.matmul(pA[:, :], att("wv"), xT[t.par][:, :], start=True, stop=True).then_inc(v_proj, 1)

            def head_sums(t, pair, of_q):
                dst = (p_den, p_cons)[pair]
                if of_q:
                    pe.wait_ge((kq1_ready, kq2_ready)[pair], t.n + 1)
                else:
                    pe.wait_ge((qk1_ready, qk2_ready)[pair], t.n + 1)
                src, at = (kq, HW) if of_q else (qk, 0)
                for s in range(SUB):
                    mm = pe.matmul(dst[:, at + s * HEADS:at + (s + 1) * HEADS], src[:, s * P:(s + 1) * P], att("headsum"),
                                   start=True, stop=True)
                mm.then_inc((den_ready, consp_ready)[pair], 1)

            def spread_T(dst, src, done):
                for s in range(SUB):
                    mm = pe.transpose(dst[:, s * P:(s + 1) * P], src[:, s * P:(s + 1) * P], ident)
                mm.then_inc(done, 1)

            def denominators_T(t, i):
                pe.wait_ge(rdenx_ready, 2 * t.n + i + 1)
                if i == 0:
                    pe.wait_ge(v_ready, t.n + 1)
                else:
                    pe.wait_ge(k_ready, t.n + 1)
                spread_T((pA, pB)[i], rden_x[:, i, :, :].rearrange("p a b -> p (a b)"), (sinkT_ready, srcT_ready)[i])

            def factor_T(t):
                pe.wait_ge(facx_ready, t.n + 1)
                pe.wait_ge(qsink_ready, t.n + 1)
                spread_T(pA, fac_x[:, :, :].rearrange("p a b -> p (a b)"), facT_ready)

            def cumulate_e(t):
                pe.wait_ge(esrc_ready, t.n + 1)
                pe.matmul(p_cume, upper, esrc[:, :], start=True, stop=False, skip_group_check=True)
                for lag in range(1, SUB):
                    mm = pe.matmul(p_cume[:, lag * HEADS:], ones, esrc[:, 0:(SUB - lag) * HEADS],
                                   start=False, stop=(lag == SUB - 1), skip_group_check=True)
                if t.par == 1:
                    pe.wait_ge(esum_ready, t.slot_uses + 1)
                    for s in range(SUB):
                        mm = pe.matmul(p_cume[:, s * HEADS:(s + 1) * HEADS], ones, esrc_sum[:, :], start=False,
                                       stop=True, skip_group_check=True)
                mm.then_inc(cume_ready, 1)

            def compensation_T(t):
                pe.wait_ge(compx_ready, t.n + 1)
                pe.wait_ge(ksrc_ready, t.n + 1)
                spread_T(pB, comp_x[:, :, :].rearrange("p a b -> p (a b)"), compT_ready)

            def reduce_out(t, m):
                pe.wait_ge(prod_ready, DH * t.n + m + 1)
                if m == 0:
                    wait(pe, res_ready[0], t.n)
                for s in range(SUB):
                    mm = pe.matmul(pO3[:, s, :], prod[:, m % 4, s * P:(s + 1) * P], s_wor[:, m, :],
                                   start=(m == 0 and s == 0), stop=(m == DH - 1), skip_group_check=True)
                mm.then_inc(red_ready, 1)

            def h_T(t):
                pe.wait_ge(norm_ready[0], SUB * (t.n + 1))
                wait(pe, hsum_ready, FC * (t.n - 2) + 3)
                for s in range(SUB):
                    mm = pe.transpose(pG[0][:, s * P:(s + 1) * P], n1[:, s, :], ident)
                mm.then_inc(hTp_ready, 1)

            def hidden(t, f):
                pe.wait_ge(hT_ready, t.n + 1)
                if f == 1:
                    wait(pe, hsum_ready, FC * (t.n - 1))
                if f >= 2:
                    pe.wait_ge(gelu_ready, FC * t.n + f - 1)
                pe.matmul(pG[f % 2][:, :], w1[:, f * P:(f + 1) * P], hT[:, :], start=True, stop=True).then_inc(w1_done, 1)

            def ffn_out(t, f):
                pe.wait_ge(gelu_ready, FC * t.n + f + 1)
                if f == 0:
                    wait(pe, res_ready[3], t.n - 1)
                for s in range(SUB):
                    mm = pe.matmul(pY3[:, s, :], gel[:, f, s * P:(s + 1) * P], w2[:, f, :],
                                   start=(f == 0 and s == 0), stop=(f == FC - 1), skip_group_check=True)
                mm.then_inc(w2_done, 1)

            def x2_T(t):
                pe.wait_ge(norm_ready[2], SUB * (t.n + 1))
                wait(pe, udT_ready, t.n)
                for s in range(SUB):
                    mm = pe.transpose(pM[:, s * P:(s + 1) * P], x2[:, s, :], ident)
                mm.then_inc(x2Tp_ready, 1)

            def logits(t):
                pe.wait_ge(x2T_ready, t.n + 1)
                for s in range(SUB):
                    mm = pe.matmul(p_log[:, s, :], x2T[t.par][:, s * P:(s + 1) * P], moe("gate"), start=True, stop=True)
                mm.then_inc(logp_ready, 1)

            def lora_in(t):
                pe.wait_ge(gate_step, GATE_STEPS * t.n + 1)
                for s in range(SUB):
                    mm = pe.matmul(pM3[:, s, :], x2T[t.par][:, s * P:(s + 1) * P], moe("la"), start=True, stop=True)
                mm.then_inc(up_ready, 1)

            def u_T(t, first_one):
                src, done = (u1, u1Tp_ready) if first_one else (ud, udTp_ready)
                if first_one:
                    pe.wait_ge(u1_ready, t.n + 1)
                    pe.wait_ge(ud_ready, t.n + 1)
                else:
                    pe.wait_ge(u1T_ready, t.n + 1)
                for s in range(SUB):
                    mm = pe.transpose(pM[:, s * P:(s + 1) * P], src[:, s, :], ident)
                mm.then_inc(done, 1)

            def inter1(t, f):
                if f == 0:
                    pe.wait_ge(x2T_ready, t.n + 1)
                    pe.wait_ge(u1T_ready, t.n + 1)
                if f < 2:
                    if t.plus(1).exists():
                        pe.wait_ge(gelu_ready, FC * (t.n + 1) + f + 3)
                    else:
                        pe.wait_ge(hsum_ready, FC * (t.n - 1) + f + 3)
                else:
                    pe.wait_ge(hsum_ready, FC * t.n + f - 1)
                pe.matmul(pG[f % 2][:, :], moe("wi")[:, f * P:(f + 1) * P], x2T[t.par][:, :], start=True, stop=False)
                pe.matmul(pG[f % 2][:, :], moe("lb")[:, f * P:(f + 1) * P], u1T[:, :], start=False, stop=True).then_inc(in1_done, 1)

            def inter2(t, f):
                if f == 0:
                    pe.wait_ge(udT_ready, t.n + 1)
                pe.wait_ge(relu_ready, FC * t.n + f + 1)
                pe.matmul(pG[f % 2][:, :], moe("lb")[:, f * P:(f + 1) * P], udT[:, :], start=False, stop=True,
                          skip_group_check=True).then_inc(in2_done, 1)

            def expert_out(t, f):
                pe.wait_ge(hsum_ready, FC * t.n + f + 1)
                if f == 0:
                    if t.plus(1).exists():
                        pe.wait_ge(res_ready[1], t.n + 2)
                    else:
                        pe.wait_ge(res_ready[3], t.n)
                for s in range(SUB):
                    mm = pe.matmul(pY3[:, s, :], hsum[:, f, s * P:(s + 1) * P], wo[:, f, :],
                                   start=(f == 0 and s == 0), stop=(f == FC - 1), skip_group_check=True)
                mm.then_inc(wo_done, 1)

            def constant_row():
                pe.wait_ge(moe_loaded, 16)
                pe.wait_ge(ones_ready, 2)
                for f in range(FC):
                    mm = pe.matmul(pM[:, 0:P], bi_rep[:, f, :], wo[:, f, :], start=(f == 0), stop=(f == FC - 1))
                mm.then_inc(cmoe_mm, 1)

            pe.wait_ge(att_loaded, 16)
            pe.wait_ge(con_loaded, 16)

            def step(s):
                a, b, c, d = s.plus(1), s, s.plus(-1), s.plus(-2)
                A, B, C, D = a.exists(), b.exists(), c.exists(), d.exists()
                if isinstance(s.n, int) and s.n == 0:
                    constant_row()
                    pe.wait_ge(y_free[0], 16)
                if isinstance(s.n, int) and s.n == 1:
                    pe.wait_ge(y_free[1], 16)
                    pe.wait_ge(cmoe_ready, 1)
                if D: u_T(d, False); inter1(d, 0); inter1(d, 1)
                if A: project_q(a); project_k(a)
                if D: inter2(d, 0); inter2(d, 1)
                if B: reduce_out(b, 0); reduce_out(b, 1)
                if D: inter1(d, 2)
                if A: project_v(a); head_sums(a, 0, True)
                if B: reduce_out(b, 2)
                if D: inter1(d, 3)
                if B: reduce_out(b, 3)
                if C: x2_T(c)
                if B: reduce_out(b, 4); reduce_out(b, 5)
                if C: logits(c)
                if A: head_sums(a, 0, False)
                if B: reduce_out(b, 6); reduce_out(b, 7)
                if D: inter2(d, 2)
                if A: denominators_T(a, 1)
                if D: inter2(d, 3)
                if C: lora_in(c)
                if D: expert_out(d, 0)
                if A: denominators_T(a, 0)
                if D: expert_out(d, 1)
                if B: h_T(b)
                if D: expert_out(d, 2)
                if A: head_sums(a, 1, False)
                if B: hidden(b, 0)
                if A: head_sums(a, 1, True)
                if B: hidden(b, 1)
                if D: expert_out(d, 3)
                if B: hidden(b, 2)
                if A: cumulate_e(a)
                if B: hidden(b, 3); ffn_out(b, 0); ffn_out(b, 1)
                if C: u_T(c, True)
                if A: compensation_T(a)
                if B: ffn_out(b, 2); ffn_out(b, 3)
                if A: factor_T(a)
            run_steps(pe, step)

        @block.scalar
        def _(act):
            def q_out(t):
                act.wait_ge(q_proj, t.n + 1)
                wait(act, qfac_ready, t.n - 1)
                act.activation(q[t.par][:, :], pA[:, :], ACT.Sigmoid, bias=col("bq")).then_inc(q_ready, 1)

            def k_out(t):
                act.wait_ge(k_proj, t.n + 1)
                wait(act, kv_ready, DH * (t.n - 1))
                act.activation(k[t.par][:, :], pB[:, :], ACT.Sigmoid, bias=col("bk")).then_inc(k_ready, 1)

            def v_out(t):
                act.wait_ge(v_proj, t.n + 1)
                wait(act, vs_ready, t.n)
                act.activation(v[:, :], pA[:, :], ACT.Identity, bias=col("bv")).then_inc(v_ready, 1)

            def spread_denominators(t, i):
                act.wait_ge(rdenn_ready, t.n + 1)
                act.activation(rden_x[:, i, :, :], rden_n[:, i * HW:(i + 1) * HW].unsqueeze(2).to_broadcast([P, HW, DH]),
                               ACT.Copy).then_inc(rdenx_ready, 1)

            def alloc_tanh(t):
                act.wait_ge(cons_ready, t.n + 1)
                act.activation(tanh_half[:, :], cons[:, 0:HW], ACT.Tanh, scale=0.5).then_inc(tanh_ready, 1)

            def source_exp(t):
                act.wait_ge(clip_ready, t.n + 1)
                if t.par == 1:
                    act.wait_ge(esum_ready, t.slot_uses + 1)
                act.activation(esrc[:, :], clipped[:, :], ACT.Exp).then_inc(esrc_ready, 1)

            def normalise3(t):
                act.wait_ge(shift3_ready, t.n + 1)
                act.wait_ge(y_free[t.par], 16 * (t.slot_uses + 1))
                for s in range(SUB):
                    act.activation(y[t.par][:, s, :], res[3][:, s, :], ACT.Identity, bias=shift3[:, s:s + 1],
                                   scale=rstd[3][:, s:s + 1]).then_inc(norm_ready[3], 1)

            def h_out(t):
                act.wait_ge(hTp_ready, t.n + 1)
                wait(act, w1_done, FC * t.n)
                act.activation(hT[:, :], pG[0][:, :], ACT.Identity, bias=col("b1n"), scale=col("g1")).then_inc(hT_ready, 1)

            def gelu(t, f):
                act.wait_ge(w1_done, FC * t.n + f + 1)
                wait(act, w2_done, FC * (t.n - 1) + f + 1)
                wait(act, wo_done, FC * (t.n - 2) + f + 1)
                act.activation(gel[:, f, :], pG[f % 2][:, :], ACT.Gelu, bias=col("b1", f)).then_inc(gelu_ready, 1)

            def x2T_out(t):
                act.wait_ge(x2Tp_ready, t.n + 1)
                act.activation(x2T[t.par][:, :], pM[:, :], ACT.Copy).then_inc(x2T_ready, 1)

            def gate_exp(t):
                act.wait_ge(gate_step, GATE_STEPS * t.n + 3)
                act.activation(ex[:, :, :], prob[:, :, :], ACT.Exp).then_inc(ex_ready, 1)

            def u1T_out(t):
                act.wait_ge(u1Tp_ready, t.n + 1)
                wait(act, in1_done, FC * t.n)
                act.activation(u1T[:, :], pM[:, :], ACT.Copy).then_inc(u1T_ready, 1)

            def udT_out(t):
                act.wait_ge(udTp_ready, t.n + 1)
                wait(act, in2_done, FC * t.n)
                act.activation(udT[:, :], pM[:, :], ACT.Copy).then_inc(udT_ready, 1)

            def relu(t, f):
                act.wait_ge(in1_done, FC * t.n + f + 1)
                act.activation(relu1[:, f % 2, :], pG[f % 2][:, :], ACT.Relu, bias=col("bi", f)).then_inc(relu_ready, 1)

            act.wait_ge(att_loaded, 16)

            def step(s):
                a, b, c, d = s.plus(1), s, s.plus(-1), s.plus(-2)
                A, B, C, D = a.exists(), b.exists(), c.exists(), d.exists()
                if D: udT_out(d); relu(d, 1)
                if A: q_out(a); k_out(a)
                if C: x2T_out(c)
                if D: relu(d, 2); relu(d, 3)
                if A: spread_denominators(a, 1)
                if C: gate_exp(c)
                if A: spread_denominators(a, 0); v_out(a)
                if B: h_out(b); gelu(b, 0)
                if A: source_exp(a)
                if B: gelu(b, 1); gelu(b, 2)
                if A: alloc_tanh(a)
                if B: gelu(b, 3)
                if C: u1T_out(c)
                if D: normalise3(d)
                if C: relu(c, 0)
            run_steps(act, step)

        @block.gpsimd
        def _(pool):
            def inverse_std(t, i):
                pool.wait_ge(mv_ready[i], SUB * (t.n + 1))
                pool.tensor_tensor(var_eps[i][:, :], mv[i][:, :, 1], con("lneps"), ALU.add).then_inc(vareps_ready[i], 1)
                pool.wait_ge(vareps_ready[i], t.n + 1)
                pool.tensor_tensor(rstd[i][:, :], var_eps[i][:, :], con("mhalf"), ALU.pow).then_inc(rstd_ready[i], 1)

            def product(t, m):
                if m == 0:
                    pool.wait_ge(qfac_ready, t.n + 1)
                pool.wait_ge(cumkv_ready, DH * t.n + m + 1)
                wait(pool, red_ready, DH * t.n + m - 3)
                pool.tensor_tensor(prod[:, m % 4, :], cum_kv[t.par][:, m, :], q_fac[t.par][:, :], ALU.mult).then_inc(prod_ready, 1)

            def attention_input(t):
                pool.wait_ge(xt_loaded[t.par], 16 * (t.slot_uses + 1))
                wait(pool, res_ready[0], t.n)
                pool.tensor_tensor(x_bo[:, :, :], xt[t.par][:, :, :], over_subs(row("bo")), ALU.add).then_inc(xbo_ready, 1)

            def shifted_x(t):
                pool.wait_ge(xt_loaded[t.par], 16 * (t.slot_uses + 1))
                wait(pool, res_ready[2], t.n)
                pool.tensor_tensor(x_b2n[:, :, :], xt[t.par][:, :, :], over_subs(row("b2n")), ALU.add).then_inc(xb2n_ready, 1)

            def scaled_h(t):
                pool.wait_ge(norm_ready[0], SUB * (t.n + 1))
                wait(pool, res_ready[1], t.n)
                pool.tensor_tensor(h_res[:, :, :], n1[:, :, :], over_subs(row("g1")), ALU.mult).then_inc(hg_ready, 1)

            def h_residual(t):
                pool.wait_ge(hg_ready, t.n + 1)
                pool.tensor_tensor(h_res[:, :, :], h_res[:, :, :], over_subs(r_b1b2[:, :]), ALU.add).then_inc(hres_ready, 1)

            def scaled_n2(t):
                pool.wait_ge(norm_ready[1], SUB * (t.n + 1))
                wait(pool, norm_ready[2], SUB * t.n)
                pool.tensor_tensor(res[2][:, :, :], n2[:, :, :], over_subs(row("g2")), ALU.mult).then_inc(zg_ready, 1)

            def outer_residual(t):
                pool.wait_ge(zg_ready, t.n + 1)
                pool.wait_ge(xb2n_ready, t.n + 1)
                pool.tensor_tensor(res[2][:, :, :], res[2][:, :, :], x_b2n[:, :, :], ALU.add).then_inc(res_ready[2], 1)

            def gated_constant(t):
                pool.wait_ge(gsum_ready, t.n + 1)
                pool.wait_ge(norm_ready[2], SUB * (t.n + 1))
                pool.tensor_tensor(c_gate[:, :, :], over_subs(r_cmoe[:, :]),
                                   gate_sum[:, :].unsqueeze(2).to_broadcast([P, SUB, P]), ALU.mult).then_inc(cg_ready, 1)

            def constant_residual(t):
                pool.wait_ge(cg_ready, t.n + 1)
                wait(pool, res_ready[3], t.n)
                pool.tensor_tensor(x2c[:, :, :], x2[:, :, :], c_gate[:, :, :], ALU.add).then_inc(x2c_ready, 1)

            def e_normal(t):
                pool.wait_ge(esrc_ready, t.n + 1)
                pool.tensor_tensor(e_norm[:, :], esrc[:, :], con("norm")[:, t.par * 2 * HW:t.par * 2 * HW + HW], ALU.mult).then_inc(enorm_ready, 1)

            def compensation(t):
                pool.wait_ge(enorm_ready, t.n + 1)
                pool.wait_ge(rcume_ready, t.n + 1)
                pool.tensor_tensor(comp_x[:, :, :], e_norm[:, :].unsqueeze(2).to_broadcast([P, HW, DH]),
                                   rcum_e[:, :].unsqueeze(2).to_broadcast([P, HW, DH]), ALU.mult).then_inc(compx_ready, 1)

            pool.memset(onesrow[:, :], 1.0).then_inc(ones_ready, 1)
            pool.wait_ge(att_loaded, 16)
            pool.wait_ge(ones_ready, 1)
            bi_cols = s_att[:, W_ATT["cols"][0] + COLS["bi"]:W_ATT["cols"][0] + COLS["bi"] + FC]
            pool.tensor_tensor(bi_rep[:, :, :], onesrow[:, :].rearrange("p (f n) -> p f n", f=FC),
                               bi_cols.unsqueeze(2).to_broadcast([P, FC, P]), ALU.mult).then_inc(ones_ready, 1)
            pool.wait_ge(row_loaded, 16)
            pool.tensor_tensor(r_b1b2[:, :], row("b1n"), row("b2"), ALU.add).then_inc(rowsum_ready, 1)
            pool.wait_ge(rowsum_ready, 1)
            pool.wait_ge(con_loaded, 16)

            def step(s):
                a, b, c, d = s.plus(1), s, s.plus(-1), s.plus(-2)
                A, B, C, D = a.exists(), b.exists(), c.exists(), d.exists()
                if isinstance(s.n, int) and s.n == 1:
                    pool.wait_ge(cmoe_ready, 1)
                if B: product(b, 0)
                if C: scaled_n2(c)
                if B: product(b, 1)
                if C: outer_residual(c)
                if B: product(b, 2); product(b, 3)
                if C: inverse_std(c, 2)
                if B: product(b, 4); product(b, 5); product(b, 6); product(b, 7)
                if A: attention_input(a)
                if B: inverse_std(b, 0); scaled_h(b)
                if A: e_normal(a)
                if B: h_residual(b)
                if A: compensation(a)
                if D: inverse_std(d, 3)
                if C: gated_constant(c)
                if B: shifted_x(b)
                if C: constant_residual(c)
                if B: inverse_std(b, 1)
            run_steps(pool, step)

        @block.vector
        def _(dve):
            scan_ones = onesrow[:, :]

            def scan(dst, src, carry):
                return dve.tensor_tensor_scan(dst, scan_ones, src, carry, ALU.mult, ALU.add)

            def carry_of(t, bufs, start):
                return start if t.par == 0 else bufs[0][:, TOK - 1:TOK]

            def cumulate_q(t):
                if t.par == 1:
                    dve.wait_ge(cumqs_ready, t.n)
                dve.wait_ge(q_ready, t.n + 1)
                scan(cum_q[t.par][:, :], q[t.par][:, :], carry_of(t, cum_q, ATT_EPS)).then_inc(cumq_ready, 1)

            def cumulate_k(t):
                dve.wait_ge(k_ready, t.n + 1)
                scan(cum_k[t.par][:, :], k[t.par][:, :], carry_of(t, cum_k, ATT_EPS)).then_inc(cumk_ready, 1)

            def k_times_cum_q(t, pair):
                dve.wait_ge((cumq_ready, cumqs_ready)[pair], t.n + 1)
                dve.wait_ge(k_ready, t.n + 1)
                dve.scalar_tensor_tensor(kq[:, :], k[t.par][:, :], ATT_EPS, (cum_q, cum_qs)[pair][t.par][:, :],
                                         ALU.add, ALU.mult).then_inc((kq1_ready, kq2_ready)[pair], 1)

            def q_times_cum_k(t, pair):
                dve.wait_ge((cumk_ready, cumks_ready)[pair], t.n + 1)
                dve.scalar_tensor_tensor(qk[:, :], q[t.par][:, :], ATT_EPS, (cum_k, cum_ks)[pair][t.par][:, :],
                                         ALU.add, ALU.mult).then_inc((qk1_ready, qk2_ready)[pair], 1)

            def inverse_denominators(t):
                dve.wait_ge(den_ready, 2 * (t.n + 1))
                dve.reciprocal(rden[:, :], p_den).then_inc(rden_ready, 1)

            def normal_denominators(t):
                dve.wait_ge(rden_ready, t.n + 1)
                at = t.par * 2 * HW
                dve.tensor_tensor(rden_n[:, :], rden[:, :], con("norm")[:, at:at + 2 * HW], ALU.mult).then_inc(rdenn_ready, 1)

            def sink(t):
                dve.wait_ge(sinkT_ready, t.n + 1)
                dve.tensor_tensor(q_sink[:, :], q[t.par][:, :], pA[:, :], ALU.mult).then_inc(qsink_ready, 1)

            def source(t):
                dve.wait_ge(srcT_ready, t.n + 1)
                dve.tensor_tensor(k_src[:, :], k[t.par][:, :], pB[:, :], ALU.mult).then_inc(ksrc_ready, 1)

            def cumulate_sink(t):
                dve.wait_ge(qsink_ready, t.n + 1)
                scan(cum_qs[t.par][:, :], q_sink[:, :], carry_of(t, cum_qs, ATT_EPS)).then_inc(cumqs_ready, 1)

            def cumulate_source(t):
                dve.wait_ge(ksrc_ready, t.n + 1)
                scan(cum_ks[t.par][:, :], k_src[:, :], carry_of(t, cum_ks, ATT_EPS)).then_inc(cumks_ready, 1)

            def conserved(t):
                dve.wait_ge(consp_ready, 2 * (t.n + 1))
                at = t.par * 2 * HW
                dve.tensor_tensor(cons[:, :], p_cons, con("inorm")[:, at:at + 2 * HW], ALU.mult).then_inc(cons_ready, 1)

            def clip_source(t):
                dve.wait_ge(cons_ready, t.n + 1)
                dve.tensor_scalar(clipped[:, :], cons[:, HW:2 * HW], -1.0, 1.0, ALU.max, ALU.min).then_inc(clip_ready, 1)

            def allocation(t):
                dve.wait_ge(tanh_ready, t.n + 1)
                dve.tensor_scalar(alloc[:, :], tanh_half[:, :], 0.5, 0.5, ALU.mult, ALU.add).then_inc(alloc_ready, 1)

            def sink_factor(t):
                dve.wait_ge(alloc_ready, t.n + 1)
                dve.tensor_tensor(fac_x[:, :, :], rden[:, 0:HW].unsqueeze(2).to_broadcast([P, HW, DH]),
                                  alloc[:, :].unsqueeze(2).to_broadcast([P, HW, DH]), ALU.mult).then_inc(facx_ready, 1)

            def sum_e(t):
                if t.par == 0:
                    dve.wait_ge(esrc_ready, t.n + 1)
                    dve.tensor_reduce(esrc_sum[:, :], esrc[:, :].rearrange("p (s h) -> p h s", s=SUB), AX_X, ALU.add).then_inc(esum_ready, 1)

            def inverse_cum_e(t):
                dve.wait_ge(cume_ready, t.n + 1)
                dve.reciprocal(rcum_e[:, :], p_cume).then_inc(rcume_ready, 1)

            def query_factor(t):
                dve.wait_ge(facT_ready, t.n + 1)
                wait(dve, prod_ready, DH * (t.n - 1))
                dve.tensor_tensor(q_fac[t.par][:, :], q[t.par][:, :], pA[:, :], ALU.mult).then_inc(qfac_ready, 1)

            def values(t):
                dve.wait_ge(compT_ready, t.n + 1)
                dve.tensor_tensor(vs[:, :], v[:, :], pB[:, :], ALU.mult).then_inc(vs_ready, 1)

            def outer_product(t, m):
                dve.wait_ge(vb_loaded[m], 16 * (t.n + 1))
                wait(dve, cumkv_ready, DH * t.n + m - 2)
                dve.tensor_tensor(kv[:, m % 3, :], k[t.par][:, :], vb[:, m, :], ALU.mult).then_inc(kv_ready, 1)

            def cumulate_kv(t, m):
                dve.wait_ge(kv_ready, DH * t.n + m + 1)
                wait(dve, prod_ready, DH * (t.n - 2) + m + 1)
                start = 0.0 if t.par == 0 else cum_kv[0][:, m, TOK - 1:TOK]
                dve.tensor_tensor_scan(cum_kv[t.par][:, m, :], scan_ones, kv[:, m % 3, :], start, ALU.mult, ALU.add).then_inc(cumkv_ready, 1)

            def moments(t, i):
                dve.wait_ge(res_ready[i], t.n + 1)
                for s in range(SUB):
                    dve.bn_stats(stats[i][:, s, :], res[i][:, s, :]).then_inc(stats_ready[i], 1)
                dve.wait_ge(stats_ready[i], SUB * (t.n + 1))
                dve.memset(fence[:, :], 0.0)
                for s in range(SUB):
                    dve.bn_aggr(mv[i][:, s, :], stats[i][:, s, :]).then_inc(mv_ready[i], 1)

            def normalise(t, i):
                dve.wait_ge(rstd_ready[i], t.n + 1)
                if i == 0:
                    wait(dve, hTp_ready, t.n)
                    wait(dve, hg_ready, t.n)
                elif i == 1:
                    wait(dve, zg_ready, t.n)
                else:
                    wait(dve, x2Tp_ready, t.n)
                    wait(dve, x2c_ready, t.n)
                dst = (n1, n2, x2)[i]
                for s in range(SUB):
                    dve.tensor_scalar(dst[:, s, :], res[i][:, s, :], mv[i][:, s, 0:1], rstd[i][:, s:s + 1],
                                      ALU.subtract, ALU.mult).then_inc(norm_ready[i], 1)

            def shift_mean3(t):
                dve.wait_ge(rstd_ready[3], t.n + 1)
                dve.scalar_tensor_tensor(shift3[:, :], mv[3][:, :, 0], -1.0, rstd[3][:, :], ALU.mult, ALU.mult).then_inc(shift3_ready, 1)

            def attention_residual(t):
                dve.wait_ge(red_ready, DH * (t.n + 1))
                dve.wait_ge(xbo_ready, t.n + 1)
                wait(dve, norm_ready[0], SUB * t.n)
                dve.tensor_tensor(res[0][:, :, :], x_bo[:, :, :], pO3, ALU.add).then_inc(res_ready[0], 1)

            def ffn_residual(t):
                dve.wait_ge(w2_done, FC * (t.n + 1))
                dve.wait_ge(hres_ready, t.n + 1)
                wait(dve, norm_ready[1], SUB * t.n)
                dve.tensor_tensor(res[1][:, :, :], h_res[:, :, :], pY3, ALU.add).then_inc(res_ready[1], 1)

            def bc(a):
                return a.unsqueeze(2).to_broadcast([P, SUB, EXPERTS])

            def gate(t, i):
                prefer = con("prefer").rearrange("p (s e) -> p s e", s=SUB)
                if i == 0:
                    dve.wait_ge(logp_ready, t.n + 1)
                elif i == 3:
                    dve.wait_ge(ex_ready, t.n + 1)
                else:
                    dve.wait_ge(gate_step, GATE_STEPS * t.n + i)
                if i == 0:
                    ins = dve.tensor_tensor(logit[:, :, :], p_log, s_gb[:, :].unsqueeze(1).to_broadcast([P, SUB, EXPERTS]), ALU.add)
                elif i == 1:
                    ins = dve.tensor_reduce(m_log[:, :], logit[:, :, :], AX_X, ALU.max)
                elif i == 2:
                    ins = dve.tensor_tensor(prob[:, :, :], logit[:, :, :], bc(m_log[:, :]), ALU.subtract)
                elif i == 3:
                    ins = dve.tensor_reduce(s_ex[:, :], ex[:, :, :], AX_X, ALU.add)
                elif i == 4:
                    ins = dve.reciprocal(r_ex[:, :], s_ex[:, :])
                elif i == 5:
                    ins = dve.tensor_tensor(prob[:, :, :], ex[:, :, :], bc(r_ex[:, :]), ALU.mult)
                elif i == 6:
                    ins = dve.tensor_reduce(top1[:, :], prob[:, :, :], AX_X, ALU.max)
                elif i == 7:
                    ins = dve.tensor_tensor(eq[:, :, :], prob[:, :, :], bc(top1[:, :]), ALU.is_equal)
                elif i == 8:
                    ins = dve.tensor_tensor(pick[:, :, :], eq[:, :, :], prefer, ALU.mult)
                elif i == 9:
                    ins = dve.tensor_reduce(m_pick[:, :], pick[:, :, :], AX_X, ALU.max)
                elif i == 10:
                    ins = dve.tensor_tensor(first[:, :, :], pick[:, :, :], bc(m_pick[:, :]), ALU.is_equal)
                elif i == 11:
                    ins = dve.scalar_tensor_tensor(prob2[:, :, :], first[:, :, :], -2.0, prob[:, :, :], ALU.mult, ALU.add)
                elif i == 12:
                    ins = dve.tensor_reduce(top2[:, :], prob2[:, :, :], AX_X, ALU.max)
                elif i == 13:
                    ins = dve.tensor_tensor(eq[:, :, :], prob2[:, :, :], bc(top2[:, :]), ALU.is_equal)
                elif i == 14:
                    ins = dve.tensor_tensor(pick[:, :, :], eq[:, :, :], prefer, ALU.mult)
                elif i == 15:
                    ins = dve.tensor_reduce(m_pick[:, :], pick[:, :, :], AX_X, ALU.max)
                elif i == 16:
                    ins = dve.tensor_tensor(second[:, :, :], pick[:, :, :], bc(m_pick[:, :]), ALU.is_equal)
                else:
                    ins = dve.tensor_tensor(delta[:, :, :], second[:, :, :], first[:, :, :], ALU.subtract)
                ins.then_inc(gate_step, 1)

            def gate_total(t):
                dve.wait_ge(gate_step, GATE_STEPS * t.n + 13)
                wait(dve, res_ready[3], t.n)
                dve.tensor_tensor(gate_sum[:, :], top1[:, :], top2[:, :], ALU.add).then_inc(gsum_ready, 1)

            def masked_lora(t, first_one):
                dve.wait_ge(up_ready, t.n + 1)
                if first_one:
                    dve.wait_ge(gate_step, GATE_STEPS * t.n + 11)
                    dst, mask, ready = u1, first, u1_ready
                else:
                    dve.wait_ge(gate_step, GATE_STEPS * (t.n + 1))
                    dst, mask, ready = ud, delta, ud_ready
                dve.tensor_tensor(dst[:, :, :].rearrange("p s (e r) -> p (s e) r", r=RANK),
                                  mask[:, :, :].rearrange("p s e -> p (s e)").unsqueeze(2).to_broadcast([P, SUB * EXPERTS, RANK]),
                                  pM[:, :].rearrange("p (a r) -> p a r", r=RANK), ALU.mult).then_inc(ready, 1)

            def second_relu(t, f):
                dve.wait_ge(in2_done, FC * t.n + f + 1)
                if t.plus(1).exists():
                    dve.wait_ge(w2_done, FC * (t.n + 1) + f + 1)
                else:
                    dve.wait_ge(wo_done, FC * (t.n - 1) + f + 1)
                dve.scalar_tensor_tensor(hsum[:, f, :], pG[f % 2][:, :], neg_bi[:, f:f + 1], relu1[:, f % 2, :],
                                         ALU.max, ALU.add).then_inc(hsum_ready, 1)

            def expert_residual(t):
                dve.wait_ge(wo_done, FC * (t.n + 1))
                dve.wait_ge(x2c_ready, t.n + 1)
                wait(dve, norm_ready[3], SUB * t.n)
                for s in range(SUB):
                    ins = dve.scalar_tensor_tensor(res[3][:, s, :], pY3[:, s, :], gate_sum[:, s:s + 1],
                                                   x2c[:, s, :], ALU.mult, ALU.add)
                ins.then_inc(res_ready[3], 1)

            dve.wait_ge(att_loaded, 16)
            bi_cols = s_att[:, W_ATT["cols"][0] + COLS["bi"]:W_ATT["cols"][0] + COLS["bi"] + FC]
            dve.tensor_scalar(neg_bi[:, :], bi_cols, -1.0, None, ALU.mult).then_inc(negbi_ready, 1)
            dve.wait_ge(negbi_ready, 1)
            dve.wait_ge(ones_ready, 1)
            dve.wait_ge(con_loaded, 16)
            dve.wait_ge(gb_loaded, 16)
            dve.wait_ge(row_loaded, 16)

            def step(s):
                a, b, c, d = s.plus(1), s, s.plus(-1), s.plus(-2)
                A, B, C, D = a.exists(), b.exists(), c.exists(), d.exists()
                if isinstance(s.n, int) and s.n == 0:
                    dve.wait_ge(cmoe_mm, 1)
                    dve.scalar_tensor_tensor(r_cmoe[:, :], row("bffn"), 2.0, pM[:, 0:P], ALU.mult, ALU.add).then_inc(cmoe_ready, 1)
                if A: cumulate_q(a)
                if B: cumulate_kv(b, 3)
                if A: k_times_cum_q(a, 0)
                if C: moments(c, 2)
                if B: outer_product(b, 5); cumulate_kv(b, 4); cumulate_kv(b, 5)
                if C: normalise(c, 2)
                if B: outer_product(b, 6)
                if A: cumulate_k(a)
                if B: cumulate_kv(b, 6); outer_product(b, 7)
                if A: q_times_cum_k(a, 0)
                if B: cumulate_kv(b, 7)
                if A: inverse_denominators(a)
                if C: gate(c, 0); gate(c, 1)
                if A: normal_denominators(a)
                if C: gate(c, 2)
                if B: attention_residual(b); moments(b, 0)
                if A: source(a)
                if D: second_relu(d, 2)
                if A: cumulate_source(a)
                if B: normalise(b, 0)
                if A: q_times_cum_k(a, 1); sink(a); cumulate_sink(a); k_times_cum_q(a, 1)
                if D: second_relu(d, 3)
                if C: gate(c, 3); gate(c, 4); gate(c, 5); gate(c, 6); gate(c, 7)
                if A: conserved(a)
                if C: gate(c, 8); gate(c, 9); gate(c, 10)
                if A: clip_source(a)
                if C: gate(c, 11); gate(c, 12); gate(c, 13); masked_lora(c, True); gate(c, 14); gate(c, 15)
                if C: gate(c, 16); gate(c, 17)
                if D: expert_residual(d)
                if C: masked_lora(c, False)
                if A: inverse_cum_e(a); allocation(a)
                if D: moments(d, 3)
                if A: sum_e(a)
                if C: gate_total(c)
                if A: sink_factor(a)
                if D: shift_mean3(d)
                if A: values(a)
                if B: ffn_residual(b)
                if A: query_factor(a)
                if B: moments(b, 1)
                if A: outer_product(a, 0); outer_product(a, 1); cumulate_kv(a, 0)
                if B: normalise(b, 1)
                if A: outer_product(a, 2); cumulate_kv(a, 1); cumulate_kv(a, 2)
                if C: second_relu(c, 0); second_relu(c, 1)
                if A: outer_product(a, 3); outer_product(a, 4)
            run_steps(dve, step)


_OUTS = [((BATCH, LENGTH, P), "float32")]


def kernel(**inputs):
    import numpy as np
    import concourse.bacc as bacc
    from concourse.bass_utils import run_bass_kernel_spmd

    a = {n[len("L0_attn_"):]: np.asarray(v) for n, v in inputs.items() if n.startswith("L0_attn_")}
    m = {n[len("L0_ffn_"):]: np.asarray(v) for n, v in inputs.items() if n.startswith("L0_ffn_")}

    def col(v):
        return v.reshape(-1, P).T

    x = a["inputs"].reshape(BATCH * LENGTH, P)
    headsum = np.kron(np.eye(HEADS), np.ones((DH, 1))).astype(np.float32)
    att_w = np.concatenate([a["Wq"], a["Wk"], a["Wv"], headsum, col(a["bq"]), col(a["bk"]), col(a["bv"]),
                            col(a["ln1_g"]), col(a["ln1_b"]), col(a["b1"]), col(m["bi"]), col(a["bq"])[:, 0:1], col(a["bq"])[:, 0:1]], axis=1)
    token = (TOK * np.arange(2)[None, :, None, None, None] + P * np.arange(SUB)[None, None, None, :, None]
             + np.arange(P)[:, None, None, None, None] + 1 + 0 * np.arange(2)[None, None, :, None, None]
             + 0 * np.arange(HEADS)[None, None, None, None, :]).astype(np.float32)
    norm = token.reshape(P, 4 * HW)
    prefer = np.tile(np.arange(EXPERTS, 0, -1), (P, SUB)).astype(np.float32)
    consts = np.concatenate([np.eye(P), np.triu(np.ones((P, P))), np.ones((P, P)), norm, 1.0 / norm, prefer,
                             np.full((P, SUB), -0.5), np.full((P, SUB), LN_EPS)], axis=1).astype(np.float32)
    wo_rep = np.repeat(a["Wo"].reshape(HEADS, 1, DH, P), DH, axis=1).reshape(P, DH, P)
    rows = np.stack([a["bo"], a["ln1_g"], a["ln1_b"], a["b2"], a["ln2_g"], a["ln2_b"], m["bo"]])
    gate_row = m["gate_b"].reshape(1, EXPERTS)

    def pieces(w):
        return w.reshape(FC, P, P).transpose(1, 0, 2).reshape(P, FF)

    ffn_w = np.concatenate([a["W1"], pieces(a["W2"])], axis=1)
    moe_w = np.concatenate([m["lora_A"].reshape(P, P).T, m["gate_w"].T, m["wi"].T,
                            m["lora_B"].transpose(0, 2, 1).reshape(P, FF), pieces(m["wo"].T)], axis=1)
    arrays = {"x": x, "x_t": x.T, "att_w": att_w, "consts": consts, "wo_rep": wo_rep, "rows": rows,
              "gate_row": gate_row, "ffn_w": ffn_w, "moe_w": moe_w}
    arrays = {n: np.ascontiguousarray(v) for n, v in arrays.items()}
    nc = bacc.Bacc("TRN2", target_bir_lowering=False, num_devices=1)
    args = [nc.dram_tensor(n, v.shape, F32, kind="ExternalInput").ap() for n, v in arrays.items()]
    out = nc.dram_tensor("out", (BATCH * LENGTH, P), F32, kind="ExternalOutput").ap()
    build(nc, *args, out)
    r = run_bass_kernel_spmd(nc, [arrays], core_ids=[0])
    return r.results[0]["out"].reshape(BATCH, LENGTH, P)
```

```python
import concourse.bass as bass
from concourse import mybir
from contextlib import ExitStack

F32 = mybir.dt.float32
ALU = mybir.AluOpType
ACT = mybir.ActivationFunctionType
AX_X = mybir.AxisListType.X

P = 128
BATCH, LENGTH = 4, 1024
HEADS, DH = 16, 8
FF = 512
EXPERTS, RANK = 8, 16
TOK = 512
SUB = TOK // P
TILES = BATCH * LENGTH // TOK
FC = FF // P
ATT_EPS = 1e-6
LN_EPS = 1e-5
WARM = (TOK, TOK)
GATE_STEPS = 18
HW = SUB * HEADS

W_ATT = {"wq": (0, 128), "wk": (128, 256), "wv": (256, 384), "headsum": (384, 400), "cols": (400, 415)}
COLS = {"bq": 0, "bk": 1, "bv": 2, "g1": 3, "b1n": 4, "b1": 5, "bi": 9}
N_COLS = 15
W_CONST = {"ident": (0, 128), "upper": (128, 256), "ones": (256, 384), "norm": (384, 640), "inorm": (640, 896),
           "prefer": (896, 928), "mhalf": (928, 932), "lneps": (932, 936), "restart": (936, 1000)}
ROWS = {"bo": 0, "g1": 1, "b1n": 2, "b2": 3, "g2": 4, "b2n": 5, "bffn": 6}
W_FFN = {"w1": (0, 512), "w2": (512, 1024)}
W_MOE = {"la": (0, 128), "gate": (128, 136), "wi": (136, 648), "lb": (648, 1160), "wo": (1160, 1672)}


class Tile:

    def __init__(self, pair, c):
        self.pair, self.c = pair, c
        self.n = 2 * pair + c
        self.par = c % 2
        self.slot_uses = pair + c // 2

    def plus(self, k):
        return Tile(self.pair, self.c + k)

    def exists(self):
        return not isinstance(self.n, int) or 0 <= self.n < TILES


def wait(eng, sem, value):
    if isinstance(value, int) and value <= 0:
        return
    eng.wait_ge(sem, value)


def run_steps(eng, step):
    for c in (-1, 0, 1, 2):
        step(Tile(0, c))
    with eng.Fori(1, 3) as pair:
        step(Tile(pair, 1))
        step(Tile(pair, 2))
    for c in (1, 2, 3):
        step(Tile(3, c))


def build(nc, x, x_t, att_w, consts, wo_rep, rows, gate_row, ffn_w, moe_w, out):
    ctx = ExitStack()
    with ctx:
        def sb(name, shape):
            return ctx.enter_context(nc.sbuf_tensor(name, shape, F32))

        def bank(name):
            return ctx.enter_context(nc.psum_tensor(name, [P, TOK], F32))

        def sem(name):
            return ctx.enter_context(nc.semaphore(name))

        s_att = sb("s_att", [P, 415])
        s_con = sb("s_con", [P, 1000])
        s_wor = sb("s_wor", [P, DH, P])
        s_row = sb("s_row", [P, 7, P])
        s_gb = sb("s_gb", [P, EXPERTS])
        s_ffn = sb("s_ffn", [P, 2 * FF])
        s_moe = sb("s_moe", [P, 1672])

        def att(name):
            return s_att[:, slice(*W_ATT[name])]

        def col(name, k=0):
            at = W_ATT["cols"][0] + COLS[name] + k
            return s_att[:, at:at + 1]

        def con(name):
            return s_con[:, slice(*W_CONST[name])]

        def moe(name):
            return s_moe[:, slice(*W_MOE[name])]

        def row(name):
            return s_row[:, ROWS[name], :]

        def by_piece(e):
            return e[:, :].rearrange("p (h s) -> p s h", s=SUB)

        def over_subs(r):
            return r.unsqueeze(1).to_broadcast([P, SUB, P])

        w1 = s_ffn[:, 0:512]
        w2 = s_ffn[:, 512:1024].rearrange("p (f n) -> p f n", f=FC)
        wo = moe("wo").rearrange("p (f n) -> p f n", f=FC)
        ident, upper, ones = con("ident"), con("upper"), con("ones")

        neg_bi = sb("neg_bi", [P, FC])
        r_b1b2 = sb("r_b1b2", [P, P])
        r_cmoe = sb("r_cmoe", [P, P])
        bi_rep = sb("bi_rep", [P, FC, P])
        onesrow = sb("onesrow", [P, TOK])

        xT = [sb(f"xT{i}", [P, TOK]) for i in range(2)]
        xt = [sb(f"xt{i}", [P, SUB, P]) for i in range(2)]
        q = [sb(f"q{i}", [P, TOK]) for i in range(2)]
        k = [sb(f"k{i}", [P, TOK]) for i in range(2)]
        v = sb("v", [P, TOK])
        cum_k = [sb(f"cum_k{i}", [P, TOK]) for i in range(2)]
        cum_q = [sb(f"cum_q{i}", [P, TOK]) for i in range(2)]
        cum_ks = [sb(f"cum_ks{i}", [P, TOK]) for i in range(2)]
        cum_qs = [sb(f"cum_qs{i}", [P, TOK]) for i in range(2)]
        qk, kq = sb("qk", [P, TOK]), sb("kq", [P, TOK])
        k_src, q_sink = sb("k_src", [P, TOK]), sb("q_sink", [P, TOK])
        rden = sb("rden", [P, 2 * HW])
        q_scale, v_scale = sb("q_scale", [P, HW]), sb("v_scale", [P, HW])
        rden_n = sb("rden_n", [P, 2 * HW])
        rden_x = sb("rden_x", [P, 2, HW, DH])
        cons = sb("cons", [P, 2 * HW])
        clipped = sb("clipped", [P, HW])
        tanh_half = sb("tanh_half", [P, HW])
        alloc = sb("alloc", [P, HW])
        fac_x = rden_x[:, 0, :, :]
        esrc = sb("esrc", [P, HW])
        e_pref = [sb(f"e_pref{i}", [P, HW]) for i in range(2)]
        rcum_e, e_norm = sb("rcum_e", [P, HW]), sb("e_norm", [P, HW])
        comp_x = rden_x[:, 1, :, :]
        q_fac = [sb(f"q_fac{i}", [P, TOK]) for i in range(2)]
        vs = sb("vs", [P, TOK])
        vb = sb("vb", [P, DH, TOK])
        kv = sb("kv", [P, 3, TOK])
        cum_kv = [sb(f"cum_kv{i}", [P, DH, TOK]) for i in range(2)]
        prod = sb("prod", [P, 4, TOK])

        x_bo = sb("x_bo", [P, SUB, P])
        x_b2n = sb("x_b2n", [P, SUB, P])
        res = [sb(f"res{i}", [P, SUB, P]) for i in range(4)]
        stats = [sb(f"stats{i}", [P, SUB, 6]) for i in range(4)]
        mv = [sb(f"mv{i}", [P, SUB, 2]) for i in range(4)]
        var_eps = [sb(f"var_eps{i}", [P, SUB]) for i in range(4)]
        rstd = [sb(f"rstd{i}", [P, SUB]) for i in range(4)]
        shift3 = sb("shift3", [P, SUB])
        fence = sb("fence", [P, 1])
        n1, n2 = sb("n1", [P, SUB, P]), sb("n2", [P, SUB, P])
        x2 = sb("x2", [P, SUB, P])
        y = [sb(f"y{i}", [P, SUB, P]) for i in range(2)]
        hT = sb("hT", [P, TOK])
        h_res = sb("h_res", [P, SUB, P])
        gel = sb("gel", [P, FC, TOK])
        hsum = gel

        x2T = [sb(f"x2T{i}", [P, TOK]) for i in range(2)]
        logit, prob, ex = (sb(n, [P, SUB, EXPERTS]) for n in ("logit", "prob", "ex"))
        prob2, eq, pick = (sb(n, [P, SUB, EXPERTS]) for n in ("prob2", "eq", "pick"))
        first, second, delta = (sb(n, [P, SUB, EXPERTS]) for n in ("first", "second", "delta"))
        m_log, s_ex, r_ex, top1, top2, m_pick = (sb(n, [P, SUB]) for n in ("m_log", "s_ex", "r_ex", "top1", "top2", "m_pick"))
        gate_sum = sb("gate_sum", [P, SUB])
        u1, ud = sb("u1", [P, SUB, P]), sb("ud", [P, SUB, P])
        u1T = sb("u1T", [P, TOK])
        udT = sb("udT", [P, TOK])
        c_gate = sb("c_gate", [P, SUB, P])
        x2c = sb("x2c", [P, SUB, P])
        relu1 = sb("relu1", [P, 2, TOK])

        pA, pB, pS, pO = bank("pA"), bank("pB"), bank("pS"), bank("pO")
        pG = [bank("pG0"), bank("pG1")]
        pY, pM = bank("pY"), bank("pM")
        pO3, pY3, pM3 = (b[:, :].rearrange("p (s n) -> p s n", s=SUB) for b in (pO, pY, pM))
        p_den, p_cons, p_cume = pS[:, 0:2 * HW], pS[:, 2 * HW:4 * HW], pS[:, 4 * HW:5 * HW]
        p_log = pM[:, 0:SUB * EXPERTS].rearrange("p (s e) -> p s e", s=SUB)

        att_loaded, con_loaded = sem("att_loaded"), sem("con_loaded")
        row_loaded, gb_loaded = sem("row_loaded"), sem("gb_loaded")
        moe_loaded = sem("moe_loaded")
        xT_loaded = [sem(f"xT_loaded{i}") for i in range(2)]
        xt_loaded = [sem(f"xt_loaded{i}") for i in range(2)]
        vb_loaded = [sem(f"vb_loaded{m}") for m in range(DH)]
        y_free = [sem(f"y_free{i}") for i in range(2)]
        ones_ready, negbi_ready, rowsum_ready, cmoe_mm, cmoe_ready = (
            sem(n) for n in ("ones_ready", "negbi_ready", "rowsum_ready", "cmoe_mm", "cmoe_ready"))
        q_proj, k_proj, v_proj = sem("q_proj"), sem("k_proj"), sem("v_proj")
        q_ready, k_ready, v_ready = sem("q_ready"), sem("k_ready"), sem("v_ready")
        cumk_ready, cumq_ready = sem("cumk_ready"), sem("cumq_ready")
        qk1_ready, kq1_ready, den_ready = sem("qk1_ready"), sem("kq1_ready"), sem("den_ready")
        rden_ready, rdenn_ready, rdenx_ready = sem("rden_ready"), sem("rdenn_ready"), sem("rdenx_ready")
        sinkT_ready, srcT_ready = sem("sinkT_ready"), sem("srcT_ready")
        qsink_ready, ksrc_ready = sem("qsink_ready"), sem("ksrc_ready")
        cumks_ready, cumqs_ready = sem("cumks_ready"), sem("cumqs_ready")
        qk2_ready, kq2_ready, consp_ready = sem("qk2_ready"), sem("kq2_ready"), sem("consp_ready")
        cons_ready, clip_ready, tanh_ready, esrc_ready = (sem(n) for n in ("cons_ready", "clip_ready", "tanh_ready", "esrc_ready"))
        alloc_ready, facx_ready, facT_ready, qfac_ready = (sem(n) for n in ("alloc_ready", "facx_ready", "facT_ready", "qfac_ready"))
        qscale_ready, vscale_ready = sem("qscale_ready"), sem("vscale_ready")
        cume_ready, rcume_ready, enorm_ready, compx_ready = (sem(n) for n in ("cume_ready", "rcume_ready", "enorm_ready", "compx_ready"))
        epref_ready = sem("epref_ready")
        compT_ready, vs_ready = sem("compT_ready"), sem("vs_ready")
        kv_ready, cumkv_ready, prod_ready, red_ready = (sem(n) for n in ("kv_ready", "cumkv_ready", "prod_ready", "red_ready"))
        res_ready = [sem(f"res_ready{i}") for i in range(4)]
        stats_ready = [sem(f"stats_ready{i}") for i in range(4)]
        mv_ready = [sem(f"mv_ready{i}") for i in range(4)]
        vareps_ready = [sem(f"vareps_ready{i}") for i in range(4)]
        rstd_ready = [sem(f"rstd_ready{i}") for i in range(4)]
        shift3_ready = sem("shift3_ready")
        norm_ready = [sem(f"norm_ready{i}") for i in range(4)]
        xbo_ready, xb2n_ready = sem("xbo_ready"), sem("xb2n_ready")
        hTp_ready, hT_ready, hg_ready, hres_ready = (sem(n) for n in ("hTp_ready", "hT_ready", "hg_ready", "hres_ready"))
        w1_done, gelu_ready, w2_done = sem("w1_done"), sem("gelu_ready"), sem("w2_done")
        zg_ready = sem("zg_ready")
        x2Tp_ready, x2T_ready, logp_ready, up_ready = (sem(n) for n in ("x2Tp_ready", "x2T_ready", "logp_ready", "up_ready"))
        gate_step = sem("gate_step")
        ex_ready = sem("ex_ready")
        gsum_ready = sem("gsum_ready")
        u1_ready, ud_ready, u1Tp_ready, udTp_ready, u1T_ready, udT_ready = (
            sem(n) for n in ("u1_ready", "ud_ready", "u1Tp_ready", "udTp_ready", "u1T_ready", "udT_ready"))
        cg_ready, x2c_ready = sem("cg_ready"), sem("x2c_ready")
        in1_done, relu_ready, in2_done, hsum_ready, wo_done = (
            sem(n) for n in ("in1_done", "relu_ready", "in2_done", "hsum_ready", "wo_done"))

        x_v = x.rearrange("(t s p) d -> p t s d", s=SUB, p=P)
        out_v = out.rearrange("(t s p) d -> p t s d", s=SUB, p=P)

        block = ctx.enter_context(nc.Block())

        @block.sync
        def _(sp):
            def load_xT(t):
                wait(sp, v_proj, t.n - 1)
                sp.dma_start(xT[t.par][:, :], x_t[:, bass.ds(t.n * TOK, TOK)]).then_inc(xT_loaded[t.par], 16)

            def load_xt(t):
                wait(sp, xbo_ready, t.n - 1)
                wait(sp, xb2n_ready, t.n - 1)
                sp.dma_start(xt[t.par][:, :, :].unsqueeze(1), x_v[:, bass.ds(t.n, 1), :, :]).then_inc(xt_loaded[t.par], 16)

            def spread_vs(t, m):
                sp.wait_ge(vs_ready, t.n + 1)
                src = vs[m:P:DH, :].unsqueeze(1).to_broadcast([HEADS, DH, TOK])
                sp.dma_start(vb[:, m, :], src).then_inc(vb_loaded[m], 16)

            def store(t):
                sp.wait_ge(norm_ready[3], SUB * (t.n + 1))
                sp.dma_start(out_v[:, bass.ds(t.n, 1), :, :], y[t.par][:, :, :].unsqueeze(1)).then_inc(y_free[t.par], 16)

            load_xT(Tile(0, 0))
            sp.dma_start(s_con[:, :], consts).then_inc(con_loaded, 16)
            load_xT(Tile(0, 1))
            sp.dma_start(s_row[:, :, :], rows.unsqueeze(0).to_broadcast([P, 7, P])).then_inc(row_loaded, 16)
            load_xt(Tile(0, 0))
            sp.dma_start(s_wor[:, :, :], wo_rep).then_inc(y_free[0], 16)
            sp.dma_start(s_ffn[:, :], ffn_w).then_inc(y_free[1], 16)
            sp.dma_start(s_moe[:, :], moe_w).then_inc(moe_loaded, 16)
            sp.dma_start(s_gb[:, :], gate_row.to_broadcast([P, EXPERTS])).then_inc(gb_loaded, 16)

            def step(s):
                a, b, c, d = s.plus(1), s, s.plus(-1), s.plus(-2)
                A, B, C, D = a.exists(), b.exists(), c.exists(), d.exists()
                if B: spread_vs(b, 4); spread_vs(b, 5); spread_vs(b, 6)
                if A and not (isinstance(a.n, int) and a.n < 2): load_xT(a)
                if A and not (isinstance(a.n, int) and a.n < 1): load_xt(a)
                if B: spread_vs(b, 7)
                if A: spread_vs(a, 0); spread_vs(a, 1)
                if D: store(d)
                if A: spread_vs(a, 2); spread_vs(a, 3)
            run_steps(sp, step)
            for i in range(2):
                sp.wait_ge(y_free[i], 16 * (TILES // 2 + 1))

        @block.tensor
        def _(pe):
            def project_q(t):
                pe.wait_ge(xT_loaded[t.par], 16 * (t.slot_uses + 1))
                wait(pe, qfac_ready, t.n)
                pe.matmul(pA[:, :], att("wq"), xT[t.par][:, :], start=True, stop=True).then_inc(q_proj, 1)

            def project_k(t):
                pe.wait_ge(xT_loaded[t.par], 16 * (t.slot_uses + 1))
                wait(pe, vs_ready, t.n)
                pe.matmul(pB[:, :], att("wk"), xT[t.par][:, :], start=True, stop=True).then_inc(k_proj, 1)

            def project_v(t):
                pe.wait_ge(q_ready, t.n + 1)
                pe.matmul(pA[:, :], att("wv"), xT[t.par][:, :], start=True, stop=True).then_inc(v_proj, 1)

            def head_sums(t, pair, of_q):
                dst = (p_den, p_cons)[pair]
                if of_q:
                    pe.wait_ge((kq1_ready, kq2_ready)[pair], t.n + 1)
                else:
                    pe.wait_ge((qk1_ready, qk2_ready)[pair], t.n + 1)
                src, at = (kq, HW) if of_q else (qk, 0)
                for s in range(SUB):
                    mm = pe.matmul(dst[:, at + s * HEADS:at + (s + 1) * HEADS], src[:, s * P:(s + 1) * P], att("headsum"),
                                   start=True, stop=True)
                mm.then_inc((den_ready, consp_ready)[pair], 1)

            def spread_T(dst, src, done):
                for s in range(SUB):
                    mm = pe.transpose(dst[:, s * P:(s + 1) * P], src[:, s * P:(s + 1) * P], ident)
                mm.then_inc(done, 1)

            def denominators_T(t, i):
                if isinstance(t.n, int) and t.n == 0:
                    pe.wait_ge(con_loaded, 16)
                pe.wait_ge(rdenx_ready, 2 * t.n + i + 1)
                if i == 0:
                    pe.wait_ge(v_ready, t.n + 1)
                else:
                    pe.wait_ge(k_ready, t.n + 1)
                spread_T((pA, pB)[i], rden_x[:, i, :, :].rearrange("p a b -> p (a b)"), (sinkT_ready, srcT_ready)[i])

            def factor_T(t):
                pe.wait_ge(facx_ready, t.n + 1)
                pe.wait_ge(qsink_ready, t.n + 1)
                spread_T(pA, fac_x[:, :, :].rearrange("p a b -> p (a b)"), facT_ready)

            def cumulate_e(t):
                pe.wait_ge(esrc_ready, t.n + 1)
                pe.matmul(p_cume, upper, by_piece(esrc), start=True, stop=False, skip_group_check=True)
                pe.wait_ge(epref_ready, t.n + 1)
                mm = pe.matmul(p_cume[:, HEADS:], ones, by_piece(e_pref[t.par])[:, 0:SUB - 1, :], start=False, stop=True, skip_group_check=True)
                if t.par == 1:
                    mm = pe.matmul(p_cume.rearrange("p (s h) -> p s h", s=SUB), ones,
                                   by_piece(e_pref[0])[:, SUB - 1, :].unsqueeze(1).to_broadcast([P, SUB, HEADS]), start=False,
                                   stop=True, skip_group_check=True)
                mm.then_inc(cume_ready, 1)

            def compensation_T(t):
                pe.wait_ge(compx_ready, t.n + 1)
                pe.wait_ge(ksrc_ready, t.n + 1)
                spread_T(pB, comp_x[:, :, :].rearrange("p a b -> p (a b)"), compT_ready)

            def reduce_out(t, m):
                pe.wait_ge(prod_ready, DH * t.n + m + 1)
                if m == 0:
                    wait(pe, res_ready[0], t.n)
                for s in range(SUB):
                    mm = pe.matmul(pO3[:, s, :], prod[:, m % 4, s * P:(s + 1) * P], s_wor[:, m, :],
                                   start=(m == 0 and s == 0), stop=(m == DH - 1), skip_group_check=True)
                mm.then_inc(red_ready, 1)

            def h_T(t):
                pe.wait_ge(norm_ready[0], SUB * (t.n + 1))
                wait(pe, hsum_ready, FC * (t.n - 2) + 3)
                for s in range(SUB):
                    mm = pe.transpose(pG[0][:, s * P:(s + 1) * P], n1[:, s, :], ident)
                mm.then_inc(hTp_ready, 1)

            def hidden(t, f):
                pe.wait_ge(hT_ready, t.n + 1)
                if f == 1:
                    wait(pe, hsum_ready, FC * (t.n - 1))
                if f >= 2:
                    pe.wait_ge(gelu_ready, FC * t.n + f - 1)
                pe.matmul(pG[f % 2][:, :], w1[:, f * P:(f + 1) * P], hT[:, :], start=True, stop=True).then_inc(w1_done, 1)

            def ffn_out(t, f):
                pe.wait_ge(gelu_ready, FC * t.n + f + 1)
                if f == 0:
                    wait(pe, res_ready[3], t.n - 1)
                for s in range(SUB):
                    mm = pe.matmul(pY3[:, s, :], gel[:, f, s * P:(s + 1) * P], w2[:, f, :],
                                   start=(f == 0 and s == 0), stop=(f == FC - 1), skip_group_check=True)
                mm.then_inc(w2_done, 1)

            def x2_T(t):
                pe.wait_ge(norm_ready[2], SUB * (t.n + 1))
                wait(pe, udT_ready, t.n)
                for s in range(SUB):
                    mm = pe.transpose(pM[:, s * P:(s + 1) * P], x2[:, s, :], ident)
                mm.then_inc(x2Tp_ready, 1)

            def logits(t):
                pe.wait_ge(x2T_ready, t.n + 1)
                for s in range(SUB):
                    mm = pe.matmul(p_log[:, s, :], x2T[t.par][:, s * P:(s + 1) * P], moe("gate"), start=True, stop=True)
                mm.then_inc(logp_ready, 1)

            def lora_in(t):
                pe.wait_ge(gate_step, GATE_STEPS * t.n + 1)
                for s in range(SUB):
                    mm = pe.matmul(pM3[:, s, :], x2T[t.par][:, s * P:(s + 1) * P], moe("la"), start=True, stop=True)
                mm.then_inc(up_ready, 1)

            def u_T(t, first_one):
                src, done = (u1, u1Tp_ready) if first_one else (ud, udTp_ready)
                if first_one:
                    pe.wait_ge(u1_ready, t.n + 1)
                    pe.wait_ge(ud_ready, t.n + 1)
                else:
                    pe.wait_ge(u1T_ready, t.n + 1)
                for s in range(SUB):
                    mm = pe.transpose(pM[:, s * P:(s + 1) * P], src[:, s, :], ident)
                mm.then_inc(done, 1)

            def inter1(t, f):
                if f == 0:
                    pe.wait_ge(x2T_ready, t.n + 1)
                    pe.wait_ge(u1T_ready, t.n + 1)
                if f < 2:
                    if t.plus(1).exists():
                        pe.wait_ge(gelu_ready, FC * (t.n + 1) + f + 3)
                    else:
                        pe.wait_ge(hsum_ready, FC * (t.n - 1) + f + 3)
                else:
                    pe.wait_ge(hsum_ready, FC * t.n + f - 1)
                pe.matmul(pG[f % 2][:, :], moe("wi")[:, f * P:(f + 1) * P], x2T[t.par][:, :], start=True, stop=False)
                pe.matmul(pG[f % 2][:, :], moe("lb")[:, f * P:(f + 1) * P], u1T[:, :], start=False, stop=True).then_inc(in1_done, 1)

            def inter2(t, f):
                if f == 0:
                    pe.wait_ge(udT_ready, t.n + 1)
                pe.wait_ge(relu_ready, FC * t.n + f + 1)
                pe.matmul(pG[f % 2][:, :], moe("lb")[:, f * P:(f + 1) * P], udT[:, :], start=False, stop=True,
                          skip_group_check=True).then_inc(in2_done, 1)

            def expert_out(t, f):
                pe.wait_ge(hsum_ready, FC * t.n + f + 1)
                if f == 0:
                    if t.plus(1).exists():
                        pe.wait_ge(res_ready[1], t.n + 2)
                    else:
                        pe.wait_ge(res_ready[3], t.n)
                for s in range(SUB):
                    mm = pe.matmul(pY3[:, s, :], hsum[:, f, s * P:(s + 1) * P], wo[:, f, :],
                                   start=(f == 0 and s == 0), stop=(f == FC - 1), skip_group_check=True)
                mm.then_inc(wo_done, 1)

            def constant_row():
                pe.wait_ge(moe_loaded, 16)
                pe.wait_ge(ones_ready, 2)
                for f in range(FC):
                    mm = pe.matmul(pM[:, 0:P], bi_rep[:, f, :], wo[:, f, :], start=(f == 0), stop=(f == FC - 1))
                mm.then_inc(cmoe_mm, 1)

            pe.wait_ge(ones_ready, 1)
            for n in WARM:
                pe.matmul(pY[:, 0:n], onesrow[:, 0:P], onesrow[:, 0:n], start=True, stop=True)
            pe.wait_ge(att_loaded, 16)

            def step(s):
                a, b, c, d = s.plus(1), s, s.plus(-1), s.plus(-2)
                A, B, C, D = a.exists(), b.exists(), c.exists(), d.exists()
                if isinstance(s.n, int) and s.n == 0:
                    constant_row()
                    pe.wait_ge(y_free[0], 16)
                if isinstance(s.n, int) and s.n == 1:
                    pe.wait_ge(y_free[1], 16)
                    pe.wait_ge(cmoe_ready, 1)
                if D: inter1(d, 2); inter1(d, 3)
                if A: project_q(a)
                if B: reduce_out(b, 1)
                if A: project_k(a)
                if D: inter2(d, 2); inter2(d, 3)
                if B: reduce_out(b, 2)
                if C: x2_T(c)
                if B: reduce_out(b, 3); reduce_out(b, 4)
                if C: logits(c)
                if B: reduce_out(b, 5); reduce_out(b, 6); reduce_out(b, 7)
                if D: expert_out(d, 0)
                if A: head_sums(a, 0, True); head_sums(a, 0, False); project_v(a)
                if D: expert_out(d, 1); expert_out(d, 2)
                if A: denominators_T(a, 0)
                if D: expert_out(d, 3)
                if B: h_T(b)
                if A: denominators_T(a, 1)
                if C: lora_in(c)
                if B: hidden(b, 0); hidden(b, 1)
                if A: head_sums(a, 1, True); head_sums(a, 1, False)
                if B: hidden(b, 2); hidden(b, 3)
                if A: cumulate_e(a)
                if B: ffn_out(b, 0)
                if C: u_T(c, True)
                if B: ffn_out(b, 1)
                if A: compensation_T(a)
                if B: ffn_out(b, 2); ffn_out(b, 3)
                if C: u_T(c, False)
                if A: factor_T(a)
                if C: inter1(c, 0); inter1(c, 1); inter2(c, 0); inter2(c, 1)
                if A: reduce_out(a, 0)
            run_steps(pe, step)

        @block.scalar
        def _(act):
            def q_out(t):
                act.wait_ge(q_proj, t.n + 1)
                wait(act, qfac_ready, t.n - 1)
                act.activation(q[t.par][:, :], pA[:, :], ACT.Sigmoid, bias=col("bq")).then_inc(q_ready, 1)

            def k_out(t):
                act.wait_ge(k_proj, t.n + 1)
                wait(act, kv_ready, DH * (t.n - 1))
                act.activation(k[t.par][:, :], pB[:, :], ACT.Sigmoid, bias=col("bk")).then_inc(k_ready, 1)

            def v_out(t):
                act.wait_ge(v_proj, t.n + 1)
                wait(act, vs_ready, t.n)
                act.activation(v[:, :], pA[:, :], ACT.Identity, bias=col("bv")).then_inc(v_ready, 1)

            def spread_denominators(t, i):
                act.wait_ge(rdenn_ready, t.n + 1)
                act.activation(rden_x[:, i, :, :], rden_n[:, i * HW:(i + 1) * HW].unsqueeze(2).to_broadcast([P, HW, DH]),
                               ACT.Copy).then_inc(rdenx_ready, 1)

            def spread_scale(t, of_q):
                act.wait_ge(qscale_ready if of_q else vscale_ready, t.n + 1)
                src, dst = (q_scale, fac_x) if of_q else (v_scale, comp_x)
                act.activation(dst[:, :, :], src[:, :].unsqueeze(2).to_broadcast([P, HW, DH]),
                               ACT.Copy).then_inc(facx_ready if of_q else compx_ready, 1)

            def alloc_tanh(t):
                act.wait_ge(cons_ready, t.n + 1)
                act.activation(tanh_half[:, :], cons[:, 0:HW], ACT.Tanh, scale=0.5).then_inc(tanh_ready, 1)

            def source_exp(t):
                act.wait_ge(clip_ready, t.n + 1)
                wait(act, epref_ready, t.n)
                act.activation(by_piece(esrc), clipped[:, :].rearrange("p (s h) -> p s h", s=SUB), ACT.Exp).then_inc(esrc_ready, 1)

            def normalise3(t):
                act.wait_ge(shift3_ready, t.n + 1)
                act.wait_ge(y_free[t.par], 16 * (t.slot_uses + 1))
                for s in range(SUB):
                    act.activation(y[t.par][:, s, :], res[3][:, s, :], ACT.Identity, bias=shift3[:, s:s + 1],
                                   scale=rstd[3][:, s:s + 1]).then_inc(norm_ready[3], 1)

            def h_out(t):
                act.wait_ge(hTp_ready, t.n + 1)
                wait(act, w1_done, FC * t.n)
                act.activation(hT[:, :], pG[0][:, :], ACT.Identity, bias=col("b1n"), scale=col("g1")).then_inc(hT_ready, 1)

            def gelu(t, f):
                act.wait_ge(w1_done, FC * t.n + f + 1)
                wait(act, w2_done, FC * (t.n - 1) + f + 1)
                wait(act, wo_done, FC * (t.n - 2) + f + 1)
                act.activation(gel[:, f, :], pG[f % 2][:, :], ACT.Gelu, bias=col("b1", f)).then_inc(gelu_ready, 1)

            def x2T_out(t):
                act.wait_ge(x2Tp_ready, t.n + 1)
                act.activation(x2T[t.par][:, :], pM[:, :], ACT.Copy).then_inc(x2T_ready, 1)

            def gate_exp(t):
                act.wait_ge(gate_step, GATE_STEPS * t.n + 3)
                act.activation(ex[:, :, :], prob[:, :, :], ACT.Exp).then_inc(ex_ready, 1)

            def gated_constant(t):
                act.wait_ge(gsum_ready, t.n + 1)
                wait(act, x2c_ready, t.n)
                for s in range(SUB):
                    ins = act.activation(c_gate[:, s, :], r_cmoe[:, :], ACT.Copy, scale=gate_sum[:, s:s + 1])
                ins.then_inc(cg_ready, 1)

            def u1T_out(t):
                act.wait_ge(u1Tp_ready, t.n + 1)
                wait(act, in1_done, FC * t.n)
                act.activation(u1T[:, :], pM[:, :], ACT.Copy).then_inc(u1T_ready, 1)

            def udT_out(t):
                act.wait_ge(udTp_ready, t.n + 1)
                wait(act, in2_done, FC * t.n)
                act.activation(udT[:, :], pM[:, :], ACT.Copy).then_inc(udT_ready, 1)

            def relu(t, f):
                act.wait_ge(in1_done, FC * t.n + f + 1)
                act.activation(relu1[:, f % 2, :], pG[f % 2][:, :], ACT.Relu, bias=col("bi", f)).then_inc(relu_ready, 1)

            act.dma_start(s_att[:, :], att_w).then_inc(att_loaded, 16)
            act.wait_ge(att_loaded, 16)

            def step(s):
                a, b, c, d = s.plus(1), s, s.plus(-1), s.plus(-2)
                A, B, C, D = a.exists(), b.exists(), c.exists(), d.exists()
                if isinstance(s.n, int) and s.n == 1:
                    act.wait_ge(cmoe_ready, 1)
                if D: relu(d, 2)
                if A: q_out(a)
                if D: relu(d, 3)
                if C: x2T_out(c)
                if A: k_out(a)
                if C: gate_exp(c)
                if A: v_out(a); spread_denominators(a, 0); spread_denominators(a, 1)
                if B: h_out(b); gelu(b, 0); gelu(b, 1)
                if A: source_exp(a); alloc_tanh(a)
                if B: gelu(b, 2)
                if A: spread_scale(a, False)
                if B: gelu(b, 3)
                if A: spread_scale(a, True)
                if C: u1T_out(c); gated_constant(c); udT_out(c)
                if D: normalise3(d)
                if C: relu(c, 0); relu(c, 1)
            run_steps(act, step)

        @block.gpsimd
        def _(pool):
            def inverse_std(t, i):
                pool.wait_ge(mv_ready[i], SUB * (t.n + 1))
                pool.tensor_tensor(var_eps[i][:, :], mv[i][:, :, 1], con("lneps"), ALU.add).then_inc(vareps_ready[i], 1)
                pool.wait_ge(vareps_ready[i], t.n + 1)
                pool.tensor_tensor(rstd[i][:, :], var_eps[i][:, :], con("mhalf"), ALU.pow).then_inc(rstd_ready[i], 1)

            def product(t, m):
                if m == 0:
                    pool.wait_ge(qfac_ready, t.n + 1)
                pool.wait_ge(cumkv_ready, DH * t.n + m + 1)
                wait(pool, red_ready, DH * t.n + m - 3)
                pool.tensor_tensor(prod[:, m % 4, :], cum_kv[t.par][:, m, :], q_fac[t.par][:, :], ALU.mult).then_inc(prod_ready, 1)

            def attention_input(t):
                pool.wait_ge(xt_loaded[t.par], 16 * (t.slot_uses + 1))
                wait(pool, res_ready[0], t.n)
                pool.tensor_tensor(x_bo[:, :, :], xt[t.par][:, :, :], over_subs(row("bo")), ALU.add).then_inc(xbo_ready, 1)

            def shifted_x(t):
                pool.wait_ge(xt_loaded[t.par], 16 * (t.slot_uses + 1))
                wait(pool, res_ready[2], t.n)
                pool.tensor_tensor(x_b2n[:, :, :], xt[t.par][:, :, :], over_subs(row("b2n")), ALU.add).then_inc(xb2n_ready, 1)

            def scaled_h(t):
                pool.wait_ge(norm_ready[0], SUB * (t.n + 1))
                wait(pool, res_ready[1], t.n)
                pool.tensor_tensor(h_res[:, :, :], n1[:, :, :], over_subs(row("g1")), ALU.mult).then_inc(hg_ready, 1)

            def h_residual(t):
                pool.wait_ge(hg_ready, t.n + 1)
                pool.tensor_tensor(h_res[:, :, :], h_res[:, :, :], over_subs(r_b1b2[:, :]), ALU.add).then_inc(hres_ready, 1)

            def scaled_n2(t):
                pool.wait_ge(norm_ready[1], SUB * (t.n + 1))
                wait(pool, norm_ready[2], SUB * t.n)
                pool.tensor_tensor(res[2][:, :, :], n2[:, :, :], over_subs(row("g2")), ALU.mult).then_inc(zg_ready, 1)

            def outer_residual(t):
                pool.wait_ge(zg_ready, t.n + 1)
                pool.wait_ge(xb2n_ready, t.n + 1)
                pool.tensor_tensor(res[2][:, :, :], res[2][:, :, :], x_b2n[:, :, :], ALU.add).then_inc(res_ready[2], 1)

            def constant_residual(t):
                pool.wait_ge(norm_ready[2], SUB * (t.n + 1))
                pool.wait_ge(cg_ready, t.n + 1)
                wait(pool, res_ready[3], t.n)
                pool.tensor_tensor(x2c[:, :, :], x2[:, :, :], c_gate[:, :, :], ALU.add).then_inc(x2c_ready, 1)

            def e_normal(t):
                pool.wait_ge(esrc_ready, t.n + 1)
                nrm = con("norm")[:, t.par * 2 * HW:t.par * 2 * HW + HW].rearrange("p (s h) -> p s h", s=SUB)
                pool.tensor_tensor(e_norm[:, :].rearrange("p (s h) -> p s h", s=SUB), by_piece(esrc), nrm, ALU.mult).then_inc(enorm_ready, 1)

            pool.memset(onesrow[:, :], 1.0).then_inc(ones_ready, 1)
            pool.wait_ge(att_loaded, 16)
            pool.wait_ge(ones_ready, 1)
            bi_cols = s_att[:, W_ATT["cols"][0] + COLS["bi"]:W_ATT["cols"][0] + COLS["bi"] + FC]
            pool.tensor_tensor(bi_rep[:, :, :], onesrow[:, :].rearrange("p (f n) -> p f n", f=FC),
                               bi_cols.unsqueeze(2).to_broadcast([P, FC, P]), ALU.mult).then_inc(ones_ready, 1)
            pool.wait_ge(row_loaded, 16)
            pool.tensor_tensor(r_b1b2[:, :], row("b1n"), row("b2"), ALU.add).then_inc(rowsum_ready, 1)
            pool.wait_ge(rowsum_ready, 1)
            pool.wait_ge(con_loaded, 16)

            def step(s):
                a, b, c, d = s.plus(1), s, s.plus(-1), s.plus(-2)
                A, B, C, D = a.exists(), b.exists(), c.exists(), d.exists()
                if C: outer_residual(c)
                if B: product(b, 1); product(b, 2)
                if C: inverse_std(c, 2)
                if B: product(b, 3); product(b, 4); product(b, 5); product(b, 6); product(b, 7); inverse_std(b, 0)
                if B: scaled_h(b)
                if A: e_normal(a); attention_input(a)
                if B: h_residual(b)
                if D: inverse_std(d, 3)
                if B: shifted_x(b)
                if C: constant_residual(c)
                if B: inverse_std(b, 1)
                if A: product(a, 0)
                if B: scaled_n2(b)
            run_steps(pool, step)

        @block.vector
        def _(dve):
            scan_ones = onesrow[:, :]

            def scan(dst, src, carry):
                return dve.tensor_tensor_scan(dst, scan_ones, src, carry, ALU.mult, ALU.add)

            def carry_of(t, bufs, start):
                return start if t.par == 0 else bufs[0][:, TOK - 1:TOK]

            def cumulate_q(t):
                if t.par == 1:
                    dve.wait_ge(cumqs_ready, t.n)
                dve.wait_ge(q_ready, t.n + 1)
                scan(cum_q[t.par][:, :], q[t.par][:, :], carry_of(t, cum_q, ATT_EPS)).then_inc(cumq_ready, 1)

            def cumulate_k(t):
                dve.wait_ge(k_ready, t.n + 1)
                scan(cum_k[t.par][:, :], k[t.par][:, :], carry_of(t, cum_k, ATT_EPS)).then_inc(cumk_ready, 1)

            def k_times_cum_q(t, pair):
                dve.wait_ge((cumq_ready, cumqs_ready)[pair], t.n + 1)
                dve.wait_ge(k_ready, t.n + 1)
                dve.scalar_tensor_tensor(kq[:, :], k[t.par][:, :], ATT_EPS, (cum_q, cum_qs)[pair][t.par][:, :],
                                         ALU.add, ALU.mult).then_inc((kq1_ready, kq2_ready)[pair], 1)

            def q_times_cum_k(t, pair):
                dve.wait_ge((cumk_ready, cumks_ready)[pair], t.n + 1)
                dve.wait_ge(q_ready, t.n + 1)
                dve.scalar_tensor_tensor(qk[:, :], q[t.par][:, :], ATT_EPS, (cum_k, cum_ks)[pair][t.par][:, :],
                                         ALU.add, ALU.mult).then_inc((qk1_ready, qk2_ready)[pair], 1)

            def inverse_denominators(t):
                dve.wait_ge(den_ready, 2 * (t.n + 1))
                dve.reciprocal(rden[:, :], p_den).then_inc(rden_ready, 1)

            def normal_denominators(t):
                dve.wait_ge(rden_ready, t.n + 1)
                if isinstance(t.n, int) and t.n == 0:
                    dve.wait_ge(con_loaded, 16)
                at = t.par * 2 * HW
                dve.tensor_tensor(rden_n[:, :], rden[:, :], con("norm")[:, at:at + 2 * HW], ALU.mult).then_inc(rdenn_ready, 1)

            def sink(t):
                dve.wait_ge(sinkT_ready, t.n + 1)
                dve.tensor_tensor(q_sink[:, :], q[t.par][:, :], pA[:, :], ALU.mult).then_inc(qsink_ready, 1)

            def source(t):
                dve.wait_ge(srcT_ready, t.n + 1)
                dve.tensor_tensor(k_src[:, :], k[t.par][:, :], pB[:, :], ALU.mult).then_inc(ksrc_ready, 1)

            def cumulate_sink(t):
                dve.wait_ge(qsink_ready, t.n + 1)
                scan(cum_qs[t.par][:, :], q_sink[:, :], carry_of(t, cum_qs, ATT_EPS)).then_inc(cumqs_ready, 1)

            def cumulate_source(t):
                dve.wait_ge(ksrc_ready, t.n + 1)
                scan(cum_ks[t.par][:, :], k_src[:, :], carry_of(t, cum_ks, ATT_EPS)).then_inc(cumks_ready, 1)

            def conserved(t):
                dve.wait_ge(consp_ready, 2 * (t.n + 1))
                at = t.par * 2 * HW
                dve.tensor_tensor(cons[:, :], p_cons, con("inorm")[:, at:at + 2 * HW], ALU.mult).then_inc(cons_ready, 1)

            def clip_source(t):
                dve.wait_ge(cons_ready, t.n + 1)
                dve.tensor_scalar(clipped[:, :], cons[:, HW:2 * HW], -1.0, 1.0, ALU.max, ALU.min).then_inc(clip_ready, 1)

            def allocation(t):
                dve.wait_ge(tanh_ready, t.n + 1)
                dve.tensor_scalar(alloc[:, :], tanh_half[:, :], 0.5, 0.5, ALU.mult, ALU.add).then_inc(alloc_ready, 1)

            def sink_factor(t):
                dve.wait_ge(alloc_ready, t.n + 1)
                dve.tensor_tensor(q_scale[:, :], rden[:, 0:HW], alloc[:, :], ALU.mult).then_inc(qscale_ready, 1)

            def source_factor(t):
                dve.wait_ge(enorm_ready, t.n + 1)
                dve.wait_ge(rcume_ready, t.n + 1)
                dve.tensor_tensor(v_scale[:, :], e_norm[:, :], rcum_e[:, :], ALU.mult).then_inc(vscale_ready, 1)

            def prefix_e(t):
                dve.wait_ge(esrc_ready, t.n + 1)
                wait(dve, cume_ready, t.n)
                dve.tensor_tensor_scan(e_pref[t.par][:, :], con("restart"), esrc[:, :], 0.0, ALU.mult, ALU.add).then_inc(epref_ready, 1)

            def inverse_cum_e(t):
                dve.wait_ge(cume_ready, t.n + 1)
                dve.reciprocal(rcum_e[:, :], p_cume).then_inc(rcume_ready, 1)

            def query_factor(t):
                dve.wait_ge(facT_ready, t.n + 1)
                wait(dve, prod_ready, DH * (t.n - 1))
                dve.tensor_tensor(q_fac[t.par][:, :], q[t.par][:, :], pA[:, :], ALU.mult).then_inc(qfac_ready, 1)

            def values(t):
                dve.wait_ge(compT_ready, t.n + 1)
                dve.tensor_tensor(vs[:, :], v[:, :], pB[:, :], ALU.mult).then_inc(vs_ready, 1)

            def outer_product(t, m):
                dve.wait_ge(vb_loaded[m], 16 * (t.n + 1))
                wait(dve, cumkv_ready, DH * t.n + m - 2)
                dve.tensor_tensor(kv[:, m % 3, :], k[t.par][:, :], vb[:, m, :], ALU.mult).then_inc(kv_ready, 1)

            def cumulate_kv(t, m):
                dve.wait_ge(kv_ready, DH * t.n + m + 1)
                wait(dve, prod_ready, DH * (t.n - 2) + m + 1)
                start = 0.0 if t.par == 0 else cum_kv[0][:, m, TOK - 1:TOK]
                dve.tensor_tensor_scan(cum_kv[t.par][:, m, :], scan_ones, kv[:, m % 3, :], start, ALU.mult, ALU.add).then_inc(cumkv_ready, 1)

            def moments(t, i):
                dve.wait_ge(res_ready[i], t.n + 1)
                for s in range(SUB):
                    dve.bn_stats(stats[i][:, s, :], res[i][:, s, :]).then_inc(stats_ready[i], 1)
                dve.wait_ge(stats_ready[i], SUB * (t.n + 1))
                dve.memset(fence[:, :], 0.0)
                for s in range(SUB):
                    dve.bn_aggr(mv[i][:, s, :], stats[i][:, s, :]).then_inc(mv_ready[i], 1)

            def normalise(t, i):
                dve.wait_ge(rstd_ready[i], t.n + 1)
                if i == 0:
                    wait(dve, hTp_ready, t.n)
                    wait(dve, hg_ready, t.n)
                elif i == 1:
                    wait(dve, zg_ready, t.n)
                else:
                    wait(dve, x2Tp_ready, t.n)
                    wait(dve, x2c_ready, t.n)
                dst = (n1, n2, x2)[i]
                for s in range(SUB):
                    dve.tensor_scalar(dst[:, s, :], res[i][:, s, :], mv[i][:, s, 0:1], rstd[i][:, s:s + 1],
                                      ALU.subtract, ALU.mult).then_inc(norm_ready[i], 1)

            def shift_mean3(t):
                dve.wait_ge(rstd_ready[3], t.n + 1)
                dve.scalar_tensor_tensor(shift3[:, :], mv[3][:, :, 0], -1.0, rstd[3][:, :], ALU.mult, ALU.mult).then_inc(shift3_ready, 1)

            def attention_residual(t):
                dve.wait_ge(red_ready, DH * (t.n + 1))
                dve.wait_ge(xbo_ready, t.n + 1)
                wait(dve, norm_ready[0], SUB * t.n)
                dve.tensor_tensor(res[0][:, :, :], x_bo[:, :, :], pO3, ALU.add).then_inc(res_ready[0], 1)

            def ffn_residual(t):
                dve.wait_ge(w2_done, FC * (t.n + 1))
                dve.wait_ge(hres_ready, t.n + 1)
                wait(dve, norm_ready[1], SUB * t.n)
                dve.tensor_tensor(res[1][:, :, :], h_res[:, :, :], pY3, ALU.add).then_inc(res_ready[1], 1)

            def bc(a):
                return a.unsqueeze(2).to_broadcast([P, SUB, EXPERTS])

            def gate(t, i):
                prefer = con("prefer").rearrange("p (s e) -> p s e", s=SUB)
                if i == 0:
                    dve.wait_ge(logp_ready, t.n + 1)
                elif i == 3:
                    dve.wait_ge(ex_ready, t.n + 1)
                else:
                    dve.wait_ge(gate_step, GATE_STEPS * t.n + i)
                if i == 0:
                    ins = dve.tensor_tensor(logit[:, :, :], p_log, s_gb[:, :].unsqueeze(1).to_broadcast([P, SUB, EXPERTS]), ALU.add)
                elif i == 1:
                    ins = dve.tensor_reduce(m_log[:, :], logit[:, :, :], AX_X, ALU.max)
                elif i == 2:
                    ins = dve.tensor_tensor(prob[:, :, :], logit[:, :, :], bc(m_log[:, :]), ALU.subtract)
                elif i == 3:
                    ins = dve.tensor_reduce(s_ex[:, :], ex[:, :, :], AX_X, ALU.add)
                elif i == 4:
                    ins = dve.reciprocal(r_ex[:, :], s_ex[:, :])
                elif i == 5:
                    ins = dve.tensor_tensor(prob[:, :, :], ex[:, :, :], bc(r_ex[:, :]), ALU.mult)
                elif i == 6:
                    ins = dve.tensor_reduce(top1[:, :], prob[:, :, :], AX_X, ALU.max)
                elif i == 7:
                    ins = dve.tensor_tensor(eq[:, :, :], prob[:, :, :], bc(top1[:, :]), ALU.is_equal)
                elif i == 8:
                    ins = dve.tensor_tensor(pick[:, :, :], eq[:, :, :], prefer, ALU.mult)
                elif i == 9:
                    ins = dve.tensor_reduce(m_pick[:, :], pick[:, :, :], AX_X, ALU.max)
                elif i == 10:
                    ins = dve.tensor_tensor(first[:, :, :], pick[:, :, :], bc(m_pick[:, :]), ALU.is_equal)
                elif i == 11:
                    ins = dve.scalar_tensor_tensor(prob2[:, :, :], first[:, :, :], -2.0, prob[:, :, :], ALU.mult, ALU.add)
                elif i == 12:
                    ins = dve.tensor_reduce(top2[:, :], prob2[:, :, :], AX_X, ALU.max)
                elif i == 13:
                    ins = dve.tensor_tensor(eq[:, :, :], prob2[:, :, :], bc(top2[:, :]), ALU.is_equal)
                elif i == 14:
                    ins = dve.tensor_tensor(pick[:, :, :], eq[:, :, :], prefer, ALU.mult)
                elif i == 15:
                    ins = dve.tensor_reduce(m_pick[:, :], pick[:, :, :], AX_X, ALU.max)
                elif i == 16:
                    ins = dve.tensor_tensor(second[:, :, :], pick[:, :, :], bc(m_pick[:, :]), ALU.is_equal)
                else:
                    ins = dve.tensor_tensor(delta[:, :, :], second[:, :, :], first[:, :, :], ALU.subtract)
                ins.then_inc(gate_step, 1)

            def gate_total(t):
                dve.wait_ge(gate_step, GATE_STEPS * t.n + 13)
                wait(dve, res_ready[3], t.n)
                dve.tensor_tensor(gate_sum[:, :], top1[:, :], top2[:, :], ALU.add).then_inc(gsum_ready, 1)

            def masked_lora(t, first_one):
                dve.wait_ge(up_ready, t.n + 1)
                if first_one:
                    dve.wait_ge(gate_step, GATE_STEPS * t.n + 11)
                    dst, mask, ready = u1, first, u1_ready
                else:
                    dve.wait_ge(gate_step, GATE_STEPS * (t.n + 1))
                    dst, mask, ready = ud, delta, ud_ready
                dve.tensor_tensor(dst[:, :, :].rearrange("p s (e r) -> p (s e) r", r=RANK),
                                  mask[:, :, :].rearrange("p s e -> p (s e)").unsqueeze(2).to_broadcast([P, SUB * EXPERTS, RANK]),
                                  pM[:, :].rearrange("p (a r) -> p a r", r=RANK), ALU.mult).then_inc(ready, 1)

            def second_relu(t, f):
                dve.wait_ge(in2_done, FC * t.n + f + 1)
                if t.plus(1).exists():
                    dve.wait_ge(w2_done, FC * (t.n + 1) + f + 1)
                else:
                    dve.wait_ge(wo_done, FC * (t.n - 1) + f + 1)
                dve.scalar_tensor_tensor(hsum[:, f, :], pG[f % 2][:, :], neg_bi[:, f:f + 1], relu1[:, f % 2, :],
                                         ALU.max, ALU.add).then_inc(hsum_ready, 1)

            def expert_residual(t):
                dve.wait_ge(wo_done, FC * (t.n + 1))
                dve.wait_ge(x2c_ready, t.n + 1)
                wait(dve, norm_ready[3], SUB * t.n)
                for s in range(SUB):
                    ins = dve.scalar_tensor_tensor(res[3][:, s, :], pY3[:, s, :], gate_sum[:, s:s + 1],
                                                   x2c[:, s, :], ALU.mult, ALU.add)
                ins.then_inc(res_ready[3], 1)

            dve.wait_ge(att_loaded, 16)
            bi_cols = s_att[:, W_ATT["cols"][0] + COLS["bi"]:W_ATT["cols"][0] + COLS["bi"] + FC]
            dve.tensor_scalar(neg_bi[:, :], bi_cols, -1.0, None, ALU.mult).then_inc(negbi_ready, 1)
            dve.wait_ge(negbi_ready, 1)
            dve.wait_ge(ones_ready, 1)

            def step(s):
                a, b, c, d = s.plus(1), s, s.plus(-1), s.plus(-2)
                A, B, C, D = a.exists(), b.exists(), c.exists(), d.exists()
                if isinstance(s.n, int) and s.n == 0:
                    dve.wait_ge(gb_loaded, 16)
                    dve.wait_ge(row_loaded, 16)
                    dve.wait_ge(cmoe_mm, 1)
                    dve.scalar_tensor_tensor(r_cmoe[:, :], row("bffn"), 2.0, pM[:, 0:P], ALU.mult, ALU.add).then_inc(cmoe_ready, 1)
                if B: outer_product(b, 4); cumulate_kv(b, 3); cumulate_kv(b, 4); outer_product(b, 5)
                if C: normalise(c, 2)
                if B: cumulate_kv(b, 5); outer_product(b, 6); cumulate_kv(b, 6); outer_product(b, 7)
                if B: cumulate_kv(b, 7)
                if A: cumulate_q(a); cumulate_k(a)
                if D: second_relu(d, 2); second_relu(d, 3)
                if A: k_times_cum_q(a, 0)
                if C: gate(c, 0)
                if A: q_times_cum_k(a, 0)
                if C: gate(c, 1)
                if B: attention_residual(b); moments(b, 0)
                if C: gate(c, 2)
                if A: inverse_denominators(a)
                if C: gate(c, 3)
                if A: normal_denominators(a)
                if C: gate(c, 4); gate(c, 5)
                if B: normalise(b, 0)
                if C: gate(c, 6); gate(c, 7)
                if A: sink(a)
                if C: gate(c, 8)
                if A: cumulate_sink(a)
                if C: gate(c, 9)
                if A: source(a); k_times_cum_q(a, 1); cumulate_source(a)
                if C: gate(c, 10)
                if A: q_times_cum_k(a, 1)
                if C: gate(c, 11); gate(c, 12); gate(c, 13)
                if D: expert_residual(d)
                if C: gate(c, 14)
                if A: conserved(a)
                if C: gate(c, 15)
                if A: clip_source(a)
                if C: masked_lora(c, True)
                if A: prefix_e(a)
                if C: gate(c, 16)
                if A: allocation(a)
                if C: gate(c, 17); gate_total(c); masked_lora(c, False)
                if A: inverse_cum_e(a); source_factor(a); sink_factor(a)
                if D: moments(d, 3)
                if A: values(a)
                if D: shift_mean3(d)
                if B: ffn_residual(b); moments(b, 1)
                if A: query_factor(a); outer_product(a, 0); cumulate_kv(a, 0)
                if B: normalise(b, 1)
                if A: outer_product(a, 1)
                if C: second_relu(c, 0); second_relu(c, 1)
                if A: outer_product(a, 2); cumulate_kv(a, 1); outer_product(a, 3); cumulate_kv(a, 2)
                if B: moments(b, 2)
            run_steps(dve, step)


_OUTS = [((BATCH, LENGTH, P), "float32")]


def kernel(**inputs):
    import numpy as np
    import concourse.bacc as bacc
    from concourse.bass_utils import run_bass_kernel_spmd

    a = {n[len("L0_attn_"):]: np.asarray(v) for n, v in inputs.items() if n.startswith("L0_attn_")}
    m = {n[len("L0_ffn_"):]: np.asarray(v) for n, v in inputs.items() if n.startswith("L0_ffn_")}

    def col(v):
        return v.reshape(-1, P).T

    x = a["inputs"].reshape(BATCH * LENGTH, P)
    headsum = np.kron(np.eye(HEADS), np.ones((DH, 1))).astype(np.float32)
    att_w = np.concatenate([a["Wq"], a["Wk"], a["Wv"], headsum, col(a["bq"]), col(a["bk"]), col(a["bv"]),
                            col(a["ln1_g"]), col(a["ln1_b"]), col(a["b1"]), col(m["bi"]), col(a["bq"])[:, 0:1], col(a["bq"])[:, 0:1]], axis=1)
    token = (TOK * np.arange(2)[None, :, None, None, None] + P * np.arange(SUB)[None, None, None, :, None]
             + np.arange(P)[:, None, None, None, None] + 1 + 0 * np.arange(2)[None, None, :, None, None]
             + 0 * np.arange(HEADS)[None, None, None, None, :]).astype(np.float32)
    norm = token.reshape(P, 4 * HW)
    prefer = np.tile(np.arange(EXPERTS, 0, -1), (P, SUB)).astype(np.float32)
    consts = np.concatenate([np.eye(P), np.triu(np.ones((P, P))), np.ones((P, P)), norm, 1.0 / norm, prefer,
                             np.full((P, SUB), -0.5), np.full((P, SUB), LN_EPS), np.tile(np.arange(SUB) > 0, (P, HEADS))], axis=1).astype(np.float32)
    wo_rep = np.repeat(a["Wo"].reshape(HEADS, 1, DH, P), DH, axis=1).reshape(P, DH, P)
    rows = np.stack([a["bo"], a["ln1_g"], a["ln1_b"], a["b2"], a["ln2_g"], a["ln2_b"], m["bo"]])
    gate_row = m["gate_b"].reshape(1, EXPERTS)

    def pieces(w):
        return w.reshape(FC, P, P).transpose(1, 0, 2).reshape(P, FF)

    ffn_w = np.concatenate([a["W1"], pieces(a["W2"])], axis=1)
    moe_w = np.concatenate([m["lora_A"].reshape(P, P).T, m["gate_w"].T, m["wi"].T,
                            m["lora_B"].transpose(0, 2, 1).reshape(P, FF), pieces(m["wo"].T)], axis=1)
    arrays = {"x": x, "x_t": x.T, "att_w": att_w, "consts": consts, "wo_rep": wo_rep, "rows": rows,
              "gate_row": gate_row, "ffn_w": ffn_w, "moe_w": moe_w}
    arrays = {n: np.ascontiguousarray(v) for n, v in arrays.items()}
    nc = bacc.Bacc("TRN2", target_bir_lowering=False, num_devices=1)
    args = [nc.dram_tensor(n, v.shape, F32, kind="ExternalInput").ap() for n, v in arrays.items()]
    out = nc.dram_tensor("out", (BATCH * LENGTH, P), F32, kind="ExternalOutput").ap()
    build(nc, *args, out)
    r = run_bass_kernel_spmd(nc, [arrays], core_ids=[0])
    return r.results[0]["out"].reshape(BATCH, LENGTH, P)
```
